# Optimizing a Trainium2 kernel written in Bass

```python
import numpy as np
import jax
import jax.numpy as jnp

def _softmax(x, axis=-1):
    return jax.nn.softmax(x, axis=axis)

def _gelu(x):
    return jax.nn.gelu(x, approximate=True)

def _silu(x):
    return jax.nn.silu(x)

def _sigmoid(x):
    return jax.nn.sigmoid(x)

def _layernorm(x, axis=-1, eps=1e-05):
    m = jnp.mean(x, axis=axis, keepdims=True)
    v = jnp.var(x, axis=axis, keepdims=True)
    return (x - m) / jnp.sqrt(v + eps)

def _scatter_add(tgt, idx, src, axis=0):
    return tgt.at[idx].add(src)

def _segment_sum(src, seg, n):
    return jax.ops.segment_sum(src, seg, n)
kernel_name = 'mk_hybrid_d1_jaxref_r4_5baa11'

def setup_inputs(seed: int=0):
    np.random.seed(seed)
    _w = jnp.asarray

    def _L0_attn_a_setup():
        import jax, jax.numpy as jnp
        import numpy as np
        LN_EPS = 1e-05

        def _s4_block(x, Wi, bi, Wf, bf, Wo, bo, Ws, bs, gamma, beta):
            i = jax.nn.sigmoid(jnp.einsum('bsd,de->bse', x, Wi) + bi)
            f = jax.nn.sigmoid(jnp.einsum('bsd,de->bse', x, Wf) + bf)
            o = jax.nn.sigmoid(jnp.einsum('bsd,de->bse', x, Wo) + bo)
            s = jnp.tanh(jnp.einsum('bsd,de->bse', x, Ws) + bs)

            def step(h, fis):
                f_t, i_t, s_t = fis
                h = f_t * h + i_t * s_t
                return (h, h)
            B, S, D = x.shape
            h0 = jnp.zeros((B, D), x.dtype)
            fT = jnp.swapaxes(f, 0, 1)
            iT = jnp.swapaxes(i, 0, 1)
            sT = jnp.swapaxes(s, 0, 1)
            _, hT = jax.lax.scan(step, h0, (fT, iT, sT))
            h = jnp.swapaxes(hT, 0, 1)
            y = o * h
            z = x + y
            mu = jnp.mean(z, axis=-1, keepdims=True)
            var = jnp.var(z, axis=-1, keepdims=True)
            return (z - mu) * jax.lax.rsqrt(var + LN_EPS) * gamma + beta
        key = jax.random.key(seed)
        ks = jax.random.split(key, 11)
        B, S, D = (8, 512, 256)
        scale = 1.0 / np.sqrt(D)
        x = jax.random.normal(ks[0], (B, S, D), dtype=jnp.float32)

        def lin(k):
            kw, kb = jax.random.split(k)
            W = jax.random.uniform(kw, (D, D), jnp.float32, -scale, scale)
            b = jax.random.uniform(kb, (D,), jnp.float32, -scale, scale)
            return (W, b)
        Wi, bi = lin(ks[1])
        Wf, bf = lin(ks[2])
        Wo, bo = lin(ks[3])
        Ws, bs = lin(ks[4])
        gamma = jnp.ones((D,), jnp.float32)
        beta = jnp.zeros((D,), jnp.float32)
        return {'x': x, 'Wi': Wi, 'bi': bi, 'Wf': Wf, 'bf': bf, 'Wo': Wo, 'bo': bo, 'Ws': Ws, 'bs': bs, 'gamma': gamma, 'beta': beta}
    _L0_attn_a_in = _L0_attn_a_setup()

    def _L0_attn_b_setup():
        import jax, jax.numpy as jnp
        import numpy as np
        import math
        B, T, D = (2, 1024, 256)
        H = 16
        HEAD_DIM = D // H
        CHUNK = 64

        def chunked_attention(q, k, v, chunk_size, scale):
            Bq, Hq, Tq, hd = q.shape
            S = k.shape[2]
            nc = Tq // chunk_size
            q_chunks = q.reshape(Bq, Hq, nc, chunk_size, hd).transpose(2, 0, 1, 3, 4)
            starts = jnp.arange(nc, dtype=jnp.int32) * chunk_size
            k_pos = jnp.arange(S)

            def body(carry, xs):
                qc, start = xs
                scores = jnp.einsum('bhqd,bhkd->bhqk', qc, k) * scale
                q_pos = start + jnp.arange(chunk_size)
                causal_mask = k_pos[None, :] > q_pos[:, None]
                scores = jnp.where(causal_mask[None, None], -jnp.inf, scores)
                m = jnp.max(scores, axis=-1, keepdims=True)
                m = jnp.where(jnp.isinf(m), jnp.zeros_like(m), m)
                p = jax.nn.softmax(scores - m, axis=-1)
                oc = jnp.einsum('bhqk,bhkd->bhqd', p, v)
                return (carry, oc)
            _, outs = jax.lax.scan(body, None, (q_chunks, starts))
            return outs.transpose(1, 2, 0, 3, 4).reshape(Bq, Hq, Tq, hd)
        key = jax.random.key(seed)
        ks = jax.random.split(key, 9)
        s = 1.0 / math.sqrt(D)
        return {'x': jax.random.normal(ks[0], (B, T, D), dtype=jnp.float32), 'Wq': jax.random.normal(ks[1], (D, D), dtype=jnp.float32) * s, 'bq': jax.random.normal(ks[2], (D,), dtype=jnp.float32) * 0.01, 'Wk': jax.random.normal(ks[3], (D, D), dtype=jnp.float32) * s, 'bk': jax.random.normal(ks[4], (D,), dtype=jnp.float32) * 0.01, 'Wv': jax.random.normal(ks[5], (D, D), dtype=jnp.float32) * s, 'bv': jax.random.normal(ks[6], (D,), dtype=jnp.float32) * 0.01, 'Wo': jax.random.normal(ks[7], (D, D), dtype=jnp.float32) * s, 'bo': jax.random.normal(ks[8], (D,), dtype=jnp.float32) * 0.01}
    _L0_attn_b_in = _L0_attn_b_setup()

    def _L0_ffn_setup():
        import jax, jax.numpy as jnp
        import numpy as np
        DIM = 256

        def _reference_tuple_inner(x, W_r, W_k, W_v, mu_r, mu_k):
            B, T, C = x.shape
            x_prev = jnp.concatenate([jnp.zeros((B, 1, C), x.dtype), x[:, :-1, :]], axis=1)
            xr = mu_r * x + (1.0 - mu_r) * x_prev
            xk = mu_k * x + (1.0 - mu_k) * x_prev
            r = jax.nn.sigmoid(jnp.einsum('btc,dc->btd', xr, W_r))
            k = jnp.einsum('btc,dc->btd', xk, W_k)
            k_act = jnp.square(jax.nn.relu(k))
            out = r * jnp.einsum('btc,dc->btd', k_act, W_v)
            new_state = x[:, -1, :]
            return (out, new_state)
        key = jax.random.key(seed)
        ks = jax.random.split(key, 6)
        B, T, C = (8, 512, DIM)
        x = jax.random.normal(ks[0], (B, T, C), dtype=jnp.float32)
        s = 1.0 / np.sqrt(C)
        W_r = jax.random.uniform(ks[1], (C, C), jnp.float32, -s, s)
        W_k = jax.random.uniform(ks[2], (C, C), jnp.float32, -s, s)
        W_v = jax.random.uniform(ks[3], (C, C), jnp.float32, -s, s)
        mu_r = jax.random.uniform(ks[4], (C,), jnp.float32)
        mu_k = jax.random.uniform(ks[5], (C,), jnp.float32)
        return {'x': x, 'W_r': W_r, 'W_k': W_k, 'W_v': W_v, 'mu_r': mu_r, 'mu_k': mu_k}
    _L0_ffn_in = _L0_ffn_setup()
    _d = {'L0_attn_a_x': _L0_attn_a_in['x'], 'L0_attn_a_Wi': _L0_attn_a_in['Wi'], 'L0_attn_a_bi': _L0_attn_a_in['bi'], 'L0_attn_a_Wf': _L0_attn_a_in['Wf'], 'L0_attn_a_bf': _L0_attn_a_in['bf'], 'L0_attn_a_Wo': _L0_attn_a_in['Wo'], 'L0_attn_a_bo': _L0_attn_a_in['bo'], 'L0_attn_a_Ws': _L0_attn_a_in['Ws'], 'L0_attn_a_bs': _L0_attn_a_in['bs'], 'L0_attn_a_gamma': _L0_attn_a_in['gamma'], 'L0_attn_a_beta': _L0_attn_a_in['beta'], 'L0_attn_b_Wq': _L0_attn_b_in['Wq'], 'L0_attn_b_bq': _L0_attn_b_in['bq'], 'L0_attn_b_Wk': _L0_attn_b_in['Wk'], 'L0_attn_b_bk': _L0_attn_b_in['bk'], 'L0_attn_b_Wv': _L0_attn_b_in['Wv'], 'L0_attn_b_bv': _L0_attn_b_in['bv'], 'L0_attn_b_Wo': _L0_attn_b_in['Wo'], 'L0_attn_b_bo': _L0_attn_b_in['bo'], 'L0_ffn_W_r': _L0_ffn_in['W_r'], 'L0_ffn_W_k': _L0_ffn_in['W_k'], 'L0_ffn_W_v': _L0_ffn_in['W_v'], 'L0_ffn_mu_r': _L0_ffn_in['mu_r'], 'L0_ffn_mu_k': _L0_ffn_in['mu_k']}
    _x0 = _d['L0_attn_a_x']
    _d['L0_attn_a_x'] = jax.random.normal(jax.random.fold_in(jax.random.key(seed), 1), (1, 4096, 256), dtype=_x0.dtype)
    del _x0
    return _d

def reference(L0_attn_a_x, L0_attn_a_Wi, L0_attn_a_bi, L0_attn_a_Wf, L0_attn_a_bf, L0_attn_a_Wo, L0_attn_a_bo, L0_attn_a_Ws, L0_attn_a_bs, L0_attn_a_gamma, L0_attn_a_beta, L0_attn_b_Wq, L0_attn_b_bq, L0_attn_b_Wk, L0_attn_b_bk, L0_attn_b_Wv, L0_attn_b_bv, L0_attn_b_Wo, L0_attn_b_bo, L0_ffn_W_r, L0_ffn_W_k, L0_ffn_W_v, L0_ffn_mu_r, L0_ffn_mu_k):

    def _L0_attn_a_ref(x, Wi, bi, Wf, bf, Wo, bo, Ws, bs, gamma, beta):
        import jax, jax.numpy as jnp
        import numpy as np
        LN_EPS = 1e-05

        def _s4_block(x, Wi, bi, Wf, bf, Wo, bo, Ws, bs, gamma, beta):
            i = jax.nn.sigmoid(jnp.einsum('bsd,de->bse', x, Wi) + bi)
            f = jax.nn.sigmoid(jnp.einsum('bsd,de->bse', x, Wf) + bf)
            o = jax.nn.sigmoid(jnp.einsum('bsd,de->bse', x, Wo) + bo)
            s = jnp.tanh(jnp.einsum('bsd,de->bse', x, Ws) + bs)

            def step(h, fis):
                f_t, i_t, s_t = fis
                h = f_t * h + i_t * s_t
                return (h, h)
            B, S, D = x.shape
            h0 = jnp.zeros((B, D), x.dtype)
            fT = jnp.swapaxes(f, 0, 1)
            iT = jnp.swapaxes(i, 0, 1)
            sT = jnp.swapaxes(s, 0, 1)
            _, hT = jax.lax.scan(step, h0, (fT, iT, sT))
            h = jnp.swapaxes(hT, 0, 1)
            y = o * h
            z = x + y
            mu = jnp.mean(z, axis=-1, keepdims=True)
            var = jnp.var(z, axis=-1, keepdims=True)
            return (z - mu) * jax.lax.rsqrt(var + LN_EPS) * gamma + beta
        return _s4_block(x, Wi, bi, Wf, bf, Wo, bo, Ws, bs, gamma, beta)

    def _L0_attn_b_ref(x, Wq, bq, Wk, bk, Wv, bv, Wo, bo):
        import jax, jax.numpy as jnp
        import numpy as np
        import math
        B, T, D = (2, 1024, 256)
        H = 16
        HEAD_DIM = D // H
        CHUNK = 64

        def chunked_attention(q, k, v, chunk_size, scale):
            Bq, Hq, Tq, hd = q.shape
            S = k.shape[2]
            nc = Tq // chunk_size
            q_chunks = q.reshape(Bq, Hq, nc, chunk_size, hd).transpose(2, 0, 1, 3, 4)
            starts = jnp.arange(nc, dtype=jnp.int32) * chunk_size
            k_pos = jnp.arange(S)

            def body(carry, xs):
                qc, start = xs
                scores = jnp.einsum('bhqd,bhkd->bhqk', qc, k) * scale
                q_pos = start + jnp.arange(chunk_size)
                causal_mask = k_pos[None, :] > q_pos[:, None]
                scores = jnp.where(causal_mask[None, None], -jnp.inf, scores)
                m = jnp.max(scores, axis=-1, keepdims=True)
                m = jnp.where(jnp.isinf(m), jnp.zeros_like(m), m)
                p = jax.nn.softmax(scores - m, axis=-1)
                oc = jnp.einsum('bhqk,bhkd->bhqd', p, v)
                return (carry, oc)
            _, outs = jax.lax.scan(body, None, (q_chunks, starts))
            return outs.transpose(1, 2, 0, 3, 4).reshape(Bq, Hq, Tq, hd)
        Bx, Tx, Dx = x.shape
        scale = 1.0 / math.sqrt(HEAD_DIM)

        def proj(W, b):
            y = x @ W.T + b
            return y.reshape(Bx, Tx, H, HEAD_DIM).transpose(0, 2, 1, 3)
        q = proj(Wq, bq)
        k = proj(Wk, bk)
        v = proj(Wv, bv)
        out = chunked_attention(q, k, v, CHUNK, scale)
        out = out.transpose(0, 2, 1, 3).reshape(Bx, Tx, Dx)
        return out @ Wo.T + bo

    def _L0_ffn_ref(x, W_r, W_k, W_v, mu_r, mu_k):
        import jax, jax.numpy as jnp
        import numpy as np
        DIM = 256

        def _reference_tuple_inner(x, W_r, W_k, W_v, mu_r, mu_k):
            B, T, C = x.shape
            x_prev = jnp.concatenate([jnp.zeros((B, 1, C), x.dtype), x[:, :-1, :]], axis=1)
            xr = mu_r * x + (1.0 - mu_r) * x_prev
            xk = mu_k * x + (1.0 - mu_k) * x_prev
            r = jax.nn.sigmoid(jnp.einsum('btc,dc->btd', xr, W_r))
            k = jnp.einsum('btc,dc->btd', xk, W_k)
            k_act = jnp.square(jax.nn.relu(k))
            out = r * jnp.einsum('btc,dc->btd', k_act, W_v)
            new_state = x[:, -1, :]
            return (out, new_state)
        return _reference_tuple_inner(x, W_r, W_k, W_v, mu_r, mu_k)[0]
    x = L0_attn_a_x
    x = x + _L0_attn_a_ref(_layernorm(x, axis=-1), L0_attn_a_Wi, L0_attn_a_bi, L0_attn_a_Wf, L0_attn_a_bf, L0_attn_a_Wo, L0_attn_a_bo, L0_attn_a_Ws, L0_attn_a_bs, L0_attn_a_gamma, L0_attn_a_beta)
    x = x + _L0_ffn_ref(_layernorm(x, axis=-1), L0_ffn_W_r, L0_ffn_W_k, L0_ffn_W_v, L0_ffn_mu_r, L0_ffn_mu_k)
    x = x + _L0_attn_b_ref(_layernorm(x, axis=-1), L0_attn_b_Wq, L0_attn_b_bq, L0_attn_b_Wk, L0_attn_b_bk, L0_attn_b_Wv, L0_attn_b_bv, L0_attn_b_Wo, L0_attn_b_bo)
    x = x + _L0_ffn_ref(_layernorm(x, axis=-1), L0_ffn_W_r, L0_ffn_W_k, L0_ffn_W_v, L0_ffn_mu_r, L0_ffn_mu_k)
    return x

_drawn_inputs = setup_inputs


def setup_inputs(seed=0):
    import zlib

    import numpy as np

    out = dict(_drawn_inputs(seed))
    spreads = {'L0_attn_a_gamma': (1.0, 0.2), 'L0_attn_a_beta': (0.0, 0.1)}
    factors = {'L0_attn_a_Wi': 2.963,
     'L0_attn_a_bi': 42.079,
     'L0_attn_a_Wf': 4.962,
     'L0_attn_a_bf': 51.506,
     'L0_attn_a_Wo': 2.991,
     'L0_attn_a_bo': 43.478,
     'L0_attn_a_bs': 6.723,
     'L0_attn_b_bq': 64.0,
     'L0_attn_b_bk': 64.0,
     'L0_attn_b_bv': 8.0,
     'L0_attn_b_bo': 8.0,
     'L0_ffn_W_r': 3.223,
     'L0_ffn_mu_r': 6.54}
    for name, (base, spread) in spreads.items():
        noise = np.random.default_rng([zlib.crc32(name.encode()), seed]).standard_normal(out[name].shape)
        drawn = base * np.exp(spread * noise) if base else spread * noise
        out[name] = jnp.asarray(drawn.astype(out[name].dtype))
    for name, factor in factors.items():
        out[name] = (out[name] * factor).astype(out[name].dtype)
    return out
```

```python
from contextlib import ExitStack

import numpy as np

import concourse.bass as bass
from concourse import mybir

F32 = mybir.dt.float32
BF16 = mybir.dt.bfloat16
ALU = mybir.AluOpType
ACT = mybir.ActivationFunctionType
AX = mybir.AxisListType

P = 128
TOKENS, DIM = 4096, 256
CHUNK = 512
CHUNKS = TOKENS // CHUNK
TT = CHUNK // P
CT = DIM // P
HEADS, HD = 16, 16
HG = 4
GROUPS = HEADS // HG
EPS = 1e-5
SCALE = HD ** -0.5
MASKED = -1e30
SLOT = CT * CHUNK

Q_PARTS = (0, 0, 1, 0, 2, 1)
K_PARTS = (0, 1, 0, 2, 0, 1)
SCORE_ROWS = HD * len(Q_PARTS)
MAX_ROWS = 3 * HG
STACK = SCORE_ROWS + MAX_ROWS
VW = HD + 1
SPAN = 1024

STEPS = [(g, c) for g in range(GROUPS) for c in range(CHUNKS)]


def first_jobs():
    order = []
    for t in range(CHUNKS + 2):
        for name, c in (("yT", t - 1), ("r", t - 2), ("k", t - 2), ("x1T", t), ("kv", t - 2), ("f", t), ("i", t),
                        ("s", t), ("o", t), ("x3T", t - 2), ("x2T", t - 1), ("q", t - 2), ("kk", t - 2),
                        ("v", t - 2)):
            if 0 <= c < CHUNKS:
                order.append((name, c))
    return order


def last_jobs():
    order = []
    for t in range(CHUNKS + 2):
        for name, c in (("x4T", t - 1), ("aT", t), ("kv", t - 2), ("proj", t), ("r", t - 1), ("k", t - 1)):
            if 0 <= c < CHUNKS:
                order.append((name, c))
    return order


def attention_order():
    LEAD = 10
    spans = []
    for s, (g, c) in enumerate(STEPS):
        for qt in range(TT):
            for h in range(HG):
                keys = (c * TT + qt + 1) * P
                for a in range(0, keys, SPAN):
                    spans.append((s, qt, h, a, min(a + SPAN, keys)))
    upto = [sum(1 for x in spans if x[0] <= s) for s in range(len(STEPS))]
    order, done, shifts = [], 0, 0
    pending = []

    def run_maxima(target):
        nonlocal done
        while done < min(target, len(spans)):
            order.append(("max", *spans[done]))
            done += 1
            if done in upto:
                pending.append([upto.index(done), 2])

    def run_shifts(upto_step=None):
        nonlocal shifts
        while pending and (pending[0][1] <= 0 or (upto_step is not None and pending[0][0] <= upto_step)):
            order.append(("shift", pending.pop(0)[0]))

    run_maxima(upto[0])
    tiles = 0
    for s, (g, c) in enumerate(STEPS):
        run_shifts(s)
        n = TT * (c + 1)
        following = (upto[s + 1] - upto[s]) if s + 1 < len(STEPS) else 0
        for j in range(n):
            target = upto[s] + LEAD + following * (j + 1) // n
            order.append(("scores", s, j, tiles, 0))
            half = done + max(0, (target - done)) // 2
            run_maxima(min(half, upto[min(s + 2, len(STEPS) - 1)]))
            order.append(("scores", s, j, tiles, 1))
            if tiles:
                order.append(("pv", tiles - 1))
            run_maxima(min(target, upto[min(s + 2, len(STEPS) - 1)]))
            if j == 1 and s:
                order.append(("out", s - 1))
            for x in pending:
                x[1] -= 1
            run_shifts()
            tiles += 1
    order.append(("pv", tiles - 1))
    order.append(("out", len(STEPS) - 1))
    return order


def build(nc, x, Wi, bi, Wf, bf, Wo_gate, bo_gate, Ws, bs, gamma, beta, WqT, bq, WkT, bk, WvT, bv, WoT, bo,
          WrT, WkfT, WvfT, mu_r, mu_k, out):
    with ExitStack() as ctx:
        def sb(name, shape, dt=F32):
            return ctx.enter_context(nc.sbuf_tensor(name, shape, dt))

        def sem(name):
            return ctx.enter_context(nc.semaphore(name))

        weights = {n: sb("w_" + n, [P, CT, DIM]) for n in
                   ("f", "i", "s", "o", "r", "k", "v", "aq", "ak", "av", "ao")}
        gamma_b, beta_b, bv_b, bo_b = (sb(n, [P, DIM]) for n in ("gamma_b", "beta_b", "bv_b", "bo_b"))
        cols = sb("cols", [P, 10, CT])
        COL = {n: k for k, n in enumerate(("f", "i", "s", "o", "aq", "ak", "mu_r", "mu_k", "om_r", "om_k"))}
        ident = sb("ident", [P, P])
        ident_b = sb("ident_b", [P, P], BF16)
        mask_b = sb("mask_b", [P, P], BF16)
        v_aug = sb("v_aug", [P, TOKENS // P, HEADS, VW])
        q_stack = sb("q_stack", [P, 3, HG, CHUNK], BF16)
        head_rows = sb("head_rows", [P, HG, CHUNK], BF16)
        stats = sb("stats", [P, TT, 6])
        mean_var = sb("mean_var", [P, 2, TT, 2])
        var_eps = sb("var_eps", [P, 2, TT])
        rstd = sb("rstd", [P, 2, TT])
        minus_half = sb("minus_half", [P, TT])
        span_max = sb("span_max", [P, 2, TT * HG, TOKENS // SPAN])
        neg_max = sb("neg_max", [P, 3, TT * HG])
        shift_parts = sb("shift_parts", [P, 2, TT * HG, 3], BF16)
        inv_sum = sb("inv_sum", [P, 2, TT, HG])

        BLK = TT * DIM
        arena = sb("arena", [P, 31 * BLK + 8])

        def blk(n, k=1):
            return arena[:, n * BLK:(n + k) * BLK]

        def tok(n):
            return blk(n).rearrange("p (t d) -> p t d", t=TT)

        def chan(n):
            return blk(n).rearrange("p (k t) -> p k t", k=CT)

        a_x = [tok(n) for n in (0, 1, 2)]
        a_xn1 = [tok(n) for n in (3, 4)]
        a_x1T = chan(5)
        a_f, a_i, a_s, a_o = (chan(n) for n in (6, 7, 8, 9))
        a_h = [chan(n) for n in (10, 11)]
        a_x1 = [tok(n) for n in (12, 13)]
        a_xn2, a_xn3 = tok(14), tok(15)
        a_xr, a_xk, a_x3T, a_k = (chan(n) for n in (16, 17, 18, 19))
        a_r = tok(20)
        a_qf, a_kf = chan(21), chan(22)
        a_qp, a_kp = (arena[:, n * BLK:n * BLK + 3 * BLK // 2].bitcast(BF16).rearrange(
            "p (r k t) -> p r k t", r=3, k=CT) for n in (23, 25))
        WT = CHUNK + 1
        a_x2T = [arena[:, 27 * BLK + b * CT * WT:27 * BLK + (b + 1) * CT * WT].rearrange(
            "p (k t) -> p k t", k=CT) for b in range(2)]
        k_stack = blk(0, 16).bitcast(BF16).rearrange("p (b h t) -> p b h t", b=2, h=HG)
        probs = blk(16, 6).rearrange("p (b h t) -> p b h t", b=3, h=HG)
        oT = blk(22).rearrange("p (b t) -> p b t", b=2)
        attn = blk(23, 8).rearrange("p (t d) -> p t d", d=DIM)
        c_x = [tok(n) for n in (0, 1, 2, 3)]
        c_aT, c_xr, c_xk, c_k = (chan(n) for n in (4, 5, 6, 7))
        c_r, c_xn4 = tok(8), tok(9)
        c_x4T = [arena[:, 10 * BLK + b * CT * WT:10 * BLK + (b + 1) * CT * WT].rearrange(
            "p (k t) -> p k t", k=CT) for b in range(2)]

        psum = ctx.enter_context(nc.psum_tensor("psum", [P, 4 * SLOT], F32))

        def slot(n):
            return psum[:, n * SLOT:(n + 1) * SLOT]

        def slot_chan(n):
            return slot(n).rearrange("p (k t) -> p k t", k=CT)

        def slot_tok(n):
            return slot(n).rearrange("p (t d) -> p t d", t=TT)

        SCORE_RING = 3
        score_bank = [psum[:, 2 * SLOT + b * CHUNK:2 * SLOT + (b + 1) * CHUNK] for b in range(SCORE_RING)]
        pv_bank = psum[:, 2 * SLOT + 3 * CHUNK:4 * SLOT]

        q_dram = nc.dram_tensor("q_parts", (3, DIM, TOKENS), BF16, kind="Internal").ap()
        k_dram = nc.dram_tensor("k_parts", (3, DIM, TOKENS), BF16, kind="Internal").ap()
        x2_dram = nc.dram_tensor("x2_rows", (TOKENS, DIM), F32, kind="Internal").ap()

        gates_loaded, rest_loaded = sem("gates_loaded"), sem("rest_loaded")
        x_loaded = [sem(f"x_loaded{b}") for b in range(3)]
        consts_ready = sem("consts_ready")
        job_full = sem("job_full")
        z_ready, i_ready, rkv_ready = sem("z_ready"), sem("i_ready"), sem("rkv_ready")
        dve_step, pool_step = sem("dve_step"), sem("pool_step")
        stats_ready, rstd_ready = sem("stats_ready"), sem("rstd_ready")
        xn1_ready, x1T_ready = sem("xn1_ready"), sem("x1T_ready")
        f_ready, s_ready, o_ready = sem("f_ready"), sem("s_ready"), sem("o_ready")
        is_ready, h_ready, y_ready = sem("is_ready"), sem("h_ready"), sem("y_ready")
        x1_ready, xn2_ready, x2T_ready = sem("x1_ready"), sem("xn2_ready"), sem("x2T_ready")
        mix_ready, r_ready, relu_ready, k2_ready = (sem(n) for n in ("mix_ready", "r_ready", "relu_ready",
                                                                     "k2_ready"))
        x2_ready, x2_stored, xn3_ready, x3T_ready = (sem(n) for n in ("x2_ready", "x2_stored", "xn3_ready",
                                                                      "x3T_ready"))
        part0_ready, rest1_ready, part1_ready, part2_ready = (sem(n) for n in (
            "part0_ready", "rest1_ready", "part1_ready", "part2_ready"))
        parts_stored, v_ready = sem("parts_stored"), sem("v_ready")
        phase_a_done, phase_b_done, pv_cleared = sem("phase_a_done"), sem("phase_b_done"), sem("pv_cleared")
        k_loaded = [sem(f"k_loaded{b}") for b in range(3)]
        q_loaded = [sem(f"q_loaded{b}") for b in range(3)]
        m_full = sem("m_full")
        span_reduced, attn_ready = sem("span_reduced"), sem("attn_ready")
        scored, exp_done, masked, pv_done = sem("scored"), sem("exp_done"), sem("masked"), sem("pv_done")
        shift_ready, shift_placed = sem("shift_ready"), sem("shift_placed")
        o_copied = sem("o_copied")
        c_loaded = [sem(f"c_loaded{b}") for b in range(4)]
        aT_ready, xn4_ready, x4T_ready = sem("aT_ready"), sem("xn4_ready"), sem("x4T_ready")
        c_mix, c_r_ready, c_relu, c_k2 = sem("c_mix"), sem("c_r_ready"), sem("c_relu"), sem("c_k2")
        c_out, stored = sem("c_out"), sem("stored")
        c_stats, c_rstd = sem("c_stats"), sem("c_rstd")
        c_full = sem("c_full")
        c_rkv, c_x3 = sem("c_rkv"), sem("c_x3")

        block = ctx.enter_context(nc.Block())

        FIRST, LAST, ORDER = first_jobs(), last_jobs(), attention_order()
        FIRST_N = {job: n for n, job in enumerate(FIRST)}
        LAST_N = {job: n for n, job in enumerate(LAST)}
        last_tile = []
        for g, c in STEPS:
            last_tile.append((last_tile[-1] if last_tile else 0) + TT * (c + 1))

        def barrier(eng, done):
            eng.drain().then_inc(done, 1)
            eng.wait_ge(done, 5)

        def rows(dram, c):
            return dram[c * CHUNK:(c + 1) * CHUNK, :].rearrange("(t p) d -> p t d", p=P)

        @block.sync
        def _(sp):
            def load_x(c):
                if c >= 3:
                    sp.wait_ge(x1_ready, c - 2)
                sp.dma_start(a_x[c % 3], rows(x, c)).then_inc(x_loaded[c % 3], 16)

            def vector(dst, v, s):
                sp.dma_start(cols[:, COL[dst], :], v.rearrange("(k p) -> p k", p=P),
                             allow_slow_non_contiguous=True).then_inc(s, 16)

            def matrix(dst, w, s):
                sp.dma_start(weights[dst][:], w.rearrange("(k p) e -> p k e", p=P)).then_inc(s, 16)

            load_x(0)
            for n, w, b in (("f", Wf, bf), ("i", Wi, bi), ("s", Ws, bs), ("o", Wo_gate, bo_gate)):
                matrix(n, w, gates_loaded)
                vector(n, b, gates_loaded)
            load_x(1)
            load_x(2)
            for n, w in (("r", WrT), ("k", WkfT), ("v", WvfT), ("aq", WqT), ("ak", WkT), ("av", WvT), ("ao", WoT)):
                matrix(n, w, rest_loaded)
            for n, v in (("aq", bq), ("ak", bk), ("mu_r", mu_r), ("mu_k", mu_k)):
                vector(n, v, rest_loaded)
            for dst, v in ((gamma_b, gamma), (beta_b, beta), (bv_b, bv), (bo_b, bo)):
                sp.dma_start(dst[:], v.partition_broadcast(P)).then_inc(rest_loaded, 16)
            for t in range(2, CHUNKS + 2):
                c = t - 2
                if t + 1 < CHUNKS:
                    load_x(t + 1)
                sp.wait_ge(x2_ready, c + 1)
                sp.dma_start(rows(x2_dram, c), a_x1[c % 2]).then_inc(x2_stored, 16)
                sp.wait_ge(part2_ready, 2 * (c + 1))
                for dram, parts in ((q_dram, a_qp), (k_dram, a_kp)):
                    for r in range(3):
                        sp.dma_start(dram[r, :, c * CHUNK:(c + 1) * CHUNK].rearrange("(k p) t -> p k t", p=P),
                                     parts[:, r]).then_inc(parts_stored, 16)
            sp.wait_ge(parts_stored, 6 * 16 * CHUNKS)
            sp.wait_ge(x2_stored, 16 * CHUNKS)
            barrier(sp, phase_a_done)

            def load_k(g, b, c0, c1):
                for i, r in enumerate(K_PARTS):
                    src = k_dram[r, g * HG * HD:(g + 1) * HG * HD, c0 * CHUNK:c1 * CHUNK]
                    sp.dma_start(k_stack[HD * i:HD * (i + 1), g % 2, :, c0 * CHUNK:c1 * CHUNK],
                                 src.rearrange("(h d) t -> d h t", d=HD)).then_inc(k_loaded[b], 16)
                if g < 2:
                    for c in range(c0, c1):
                        sp.dma_start(k_stack[SCORE_ROWS:STACK, g % 2, :, c * CHUNK:(c + 1) * CHUNK],
                                     head_rows[SCORE_ROWS:STACK]).then_inc(k_loaded[b], 16)

            def load_q(s):
                g, c = STEPS[s]
                if s >= 3:
                    sp.wait_ge(scored, HG * last_tile[s - 3])
                for i, r in enumerate(Q_PARTS):
                    src = q_dram[r, g * HG * HD:(g + 1) * HG * HD, c * CHUNK:(c + 1) * CHUNK]
                    sp.dma_start(q_stack[HD * i:HD * (i + 1), s % 3],
                                 src.rearrange("(h d) t -> d h t", d=HD)).then_inc(q_loaded[s % 3], 16)

            load_k(0, 0, 0, 1)
            load_q(0)
            load_q(1)
            load_k(0, 1, 1, CHUNKS)
            load_q(2)
            for s in range(len(STEPS)):
                if s % CHUNKS == 0 and s // CHUNKS + 1 < GROUPS:
                    if s:
                        sp.wait_ge(scored, HG * last_tile[s - 1])
                    load_k(s // CHUNKS + 1, 2 if s == 0 else (s // CHUNKS + 1) % 2, 0, CHUNKS)
                if s + 3 < len(STEPS):
                    load_q(s + 3)
            barrier(sp, phase_b_done)

            def load_c(c):
                if c >= 4:
                    sp.wait_ge(stored, 16 * (c - 3))
                sp.dma_start(c_x[c % 4], rows(x2_dram, c)).then_inc(c_loaded[c % 4], 16)

            for c in range(4):
                load_c(c)
            for c in range(CHUNKS):
                sp.wait_ge(c_out, c + 1)
                sp.dma_start(rows(out, c), c_x[c % 4]).then_inc(stored, 16)
                if c + 4 < CHUNKS:
                    load_c(c + 4)
            sp.wait_ge(stored, 16 * CHUNKS)

        @block.gpsimd
        def _(pool):
            steps = [0]

            def settle(ins):
                steps[0] += 1
                ins.then_inc(pool_step, 1)
                pool.wait_ge(pool_step, steps[0])

            lns = [0]

            def rstd_of(ready, done, first):
                n = lns[0]
                lns[0] += 1
                pool.wait_ge(ready, n - first + 1)
                settle(nc.gpsimd.tensor_scalar(var_eps[:, n % 2, :], mean_var[:, n % 2, :, 1], EPS, None, ALU.add))
                nc.gpsimd.tensor_tensor(rstd[:, n % 2, :], var_eps[:, n % 2, :], minus_half[:],
                                        ALU.pow).then_inc(done, 1)

            settle(nc.gpsimd.memset(minus_half[:], -0.5))
            rstd_of(stats_ready, rstd_ready, 0)
            ready = [0]

            def const(ins):
                ready[0] += 1
                ins.then_inc(consts_ready, 1)
                pool.wait_ge(consts_ready, ready[0])

            for m in (ident, ident_b):
                settle(nc.gpsimd.memset(m[:], 0.0))
                const(nc.gpsimd.affine_select(out=m[:], in_=m[:], compare_op=ALU.not_equal, fill=1.0, base=0,
                                              pattern=[[-1, P]], channel_multiplier=1))
            settle(nc.gpsimd.memset(mask_b[:], 0.0))
            const(nc.gpsimd.affine_select(out=mask_b[:], in_=mask_b[:], compare_op=ALU.is_ge, fill=MASKED, base=0,
                                          pattern=[[-1, P]], channel_multiplier=1))
            settle(nc.gpsimd.memset(a_x2T[0][:, :, 0:1], 0.0))
            hr = head_rows[SCORE_ROWS:STACK]
            settle(nc.gpsimd.memset(hr, 1.0))
            settle(nc.gpsimd.affine_select(out=hr, in_=hr, compare_op=ALU.is_ge, fill=0.0, base=0,
                                           pattern=[[-3, HG], [0, CHUNK]], channel_multiplier=1))
            const(nc.gpsimd.affine_select(out=hr, in_=hr, compare_op=ALU.is_ge, fill=0.0, base=2,
                                          pattern=[[3, HG], [0, CHUNK]], channel_multiplier=-1))
            const(nc.gpsimd.memset(v_aug[:], 1.0))

            for t in range(CHUNKS + 2):
                if 0 <= t - 1 < CHUNKS:
                    rstd_of(stats_ready, rstd_ready, 0)
                    rstd_of(stats_ready, rstd_ready, 0)
                if 0 <= t - 2 < CHUNKS:
                    pool.wait_ge(relu_ready, t - 1)
                    nc.gpsimd.tensor_tensor(a_k[:], a_k[:], a_k[:], ALU.mult).then_inc(k2_ready, 1)
                    rstd_of(stats_ready, rstd_ready, 0)
                if t < CHUNKS:
                    pool.wait_ge(s_ready, t + 1)
                    nc.gpsimd.tensor_tensor(a_i[:], a_i[:], a_s[:], ALU.mult).then_inc(is_ready, 1)
                    pool.wait_ge(h_ready, t + 1)
                    pool.wait_ge(o_ready, t + 1)
                    nc.gpsimd.tensor_tensor(a_o[:], a_o[:], a_h[t % 2], ALU.mult).then_inc(y_ready, 1)
                if 0 <= t - 2 < CHUNKS:
                    for n, (rest, parts) in enumerate(((a_qf, a_qp), (a_kf, a_kp))):
                        pool.wait_ge(part1_ready, 2 * (t - 2) + n + 1)
                        nc.gpsimd.tensor_tensor(parts[:, 2], rest, parts[:, 1],
                                                ALU.subtract).then_inc(part2_ready, 1)
                if t + 1 < CHUNKS:
                    rstd_of(stats_ready, rstd_ready, 0)
            first_lns = lns[0]
            barrier(pool, phase_a_done)

            for item in ORDER:
                if item[0] == "scores" and item[4] == 1:
                    _, s, j, tile, _ = item
                    g, c = STEPS[s]
                    d = j - c * TT
                    if d >= 0:
                        pool.wait_ge(exp_done, HG * (tile + 1))
                        tri = probs[:, tile % 3, :, d * P:(d + 1) * P]
                        nc.gpsimd.affine_select(out=tri, in_=tri, compare_op=ALU.is_ge, fill=0.0, base=0,
                                                pattern=[[0, HG], [1, P]],
                                                channel_multiplier=-1).then_inc(masked, 1)
            barrier(pool, phase_b_done)

            const(nc.gpsimd.memset(c_x4T[0][:, :, 0:1], 0.0))
            for t in range(CHUNKS + 2):
                if t < CHUNKS:
                    rstd_of(c_stats, c_rstd, first_lns)
                if 0 <= t - 1 < CHUNKS:
                    pool.wait_ge(c_relu, t)
                    nc.gpsimd.tensor_tensor(c_k[:], c_k[:], c_k[:], ALU.mult).then_inc(c_k2, 1)

        @block.scalar
        def _(act):
            def take(name, c):
                n = FIRST_N[name, c]
                act.wait_ge(job_full, n + 1)
                return n % 4

            for t in range(CHUNKS + 2):
                a, b, c = t, t - 1, t - 2
                if 0 <= c < CHUNKS:
                    n = take("r", c)
                    if c:
                        act.wait_ge(x2_ready, c)
                    act.activation(a_r, slot_tok(n), ACT.Sigmoid).then_inc(r_ready, 1)
                    n = take("k", c)
                    act.activation(a_k, slot_chan(n), ACT.Relu).then_inc(relu_ready, 1)
                if a < CHUNKS:
                    n = take("x1T", a)
                    act.activation(a_x1T, slot_chan(n), ACT.Copy).then_inc(x1T_ready, 1)
                    if a:
                        act.wait_ge(h_ready, a)
                    n = take("f", a)
                    act.wait_ge(gates_loaded, 16 * 8)
                    for k in range(CT):
                        ins = act.activation(a_f[:, k], slot_chan(n)[:, k], ACT.Sigmoid,
                                             bias=cols[:, COL["f"], k:k + 1])
                    ins.then_inc(f_ready, 1)
                    n = take("i", a)
                    for k in range(CT):
                        ins = act.activation(a_i[:, k], slot_chan(n)[:, k], ACT.Sigmoid,
                                             bias=cols[:, COL["i"], k:k + 1])
                    ins.then_inc(i_ready, 1)
                    n = take("s", a)
                    for k in range(CT):
                        ins = act.activation(a_s[:, k], slot_chan(n)[:, k], ACT.Tanh,
                                             bias=cols[:, COL["s"], k:k + 1])
                    ins.then_inc(s_ready, 1)
                    n = take("o", a)
                    for k in range(CT):
                        ins = act.activation(a_o[:, k], slot_chan(n)[:, k], ACT.Sigmoid,
                                             bias=cols[:, COL["o"], k:k + 1])
                    ins.then_inc(o_ready, 1)
                if 0 <= c < CHUNKS:
                    n = take("x3T", c)
                    act.activation(a_x3T, slot_chan(n), ACT.Copy).then_inc(x3T_ready, 1)
                if 0 <= b < CHUNKS:
                    n = take("x2T", b)
                    if b:
                        act.wait_ge(mix_ready, b)
                    act.activation(a_x2T[(b + 1) % 2][:, :, 0:1], slot_chan(n)[:, :, CHUNK - 1:CHUNK], ACT.Copy)
                    act.activation(a_x2T[b % 2][:, :, 1:], slot_chan(n), ACT.Copy).then_inc(x2T_ready, 1)
                if 0 <= c < CHUNKS:
                    if c == 0:
                        act.wait_ge(rest_loaded, 16 * 15)
                    else:
                        act.wait_ge(parts_stored, 6 * 16 * c)
                    for m, (name, bias, full, parts) in enumerate((("q", "aq", a_qf, a_qp),
                                                                   ("kk", "ak", a_kf, a_kp))):
                        n = take(name, c)
                        for k in range(CT):
                            bias_k = cols[:, COL[bias], k:k + 1]
                            act.activation(full[:, k], slot_chan(n)[:, k], ACT.Identity, bias=bias_k)
                            ins = act.activation(parts[:, 0, k], slot_chan(n)[:, k], ACT.Identity, bias=bias_k)
                        ins.then_inc(part0_ready, 1)
                    for m, (full, parts) in enumerate(((a_qf, a_qp), (a_kf, a_kp))):
                        act.wait_ge(rest1_ready, 2 * c + m + 1)
                        act.activation(parts[:, 1], full, ACT.Copy).then_inc(part1_ready, 1)
            barrier(act, phase_a_done)

            jobs = 0
            tiles = 0
            for item in ORDER:
                if item[0] == "max":
                    jobs += 1
                elif item[0] == "shift":
                    s = item[1]
                    act.wait_ge(m_full, jobs + 1)
                    src = slot(jobs % 2)[SCORE_ROWS:STACK, 0:CHUNK]
                    for h in range(HG):
                        ins = act.activation(q_stack[SCORE_ROWS:STACK, s % 3, h], src, ACT.Copy)
                    ins.then_inc(shift_placed, 1)
                    jobs += 1
                elif item[0] == "scores":
                    _, s, j, tile, half = item
                    g, c = STEPS[s]
                    q0 = max(0, j - c * TT) * P
                    for h in range(half * 2, half * 2 + 2):
                        act.wait_ge(scored, tiles + 1)
                        if h == 0 and tile >= 3:
                            act.wait_ge(pv_done, tile - 2)
                        act.activation(probs[:, tile % 3, h, q0:], score_bank[tiles % SCORE_RING][:, q0:],
                                       ACT.Exp, scale=SCALE).then_inc(exp_done, 1)
                        tiles += 1
                elif item[0] == "pv" and item[1] + 1 in last_tile:
                    s = last_tile.index(item[1] + 1)
                    act.wait_ge(pv_done, item[1] + 1)
                    act.activation(oT[:, s % 2], pv_bank, ACT.Copy).then_inc(o_copied, 1)
                elif item[0] == "out":
                    jobs += 1
            barrier(act, phase_b_done)

            def c_take(name, c):
                n = LAST_N[name, c]
                act.wait_ge(c_full, n + 1)
                return n % 4

            for t in range(CHUNKS + 2):
                b = t - 1
                if 0 <= b < CHUNKS:
                    n = c_take("x4T", b)
                    if b:
                        act.wait_ge(c_mix, b)
                    act.activation(c_x4T[(b + 1) % 2][:, :, 0:1], slot_chan(n)[:, :, CHUNK - 1:CHUNK], ACT.Copy)
                    act.activation(c_x4T[b % 2][:, :, 1:], slot_chan(n), ACT.Copy).then_inc(x4T_ready, 1)
                if t < CHUNKS:
                    n = c_take("aT", t)
                    act.activation(c_aT, slot_chan(n), ACT.Copy).then_inc(aT_ready, 1)
                if 0 <= b < CHUNKS:
                    n = c_take("r", b)
                    if b:
                        act.wait_ge(c_out, b)
                    act.activation(c_r, slot_tok(n), ACT.Sigmoid).then_inc(c_r_ready, 1)
                    n = c_take("k", b)
                    act.activation(c_k, slot_chan(n), ACT.Relu).then_inc(c_relu, 1)

        @block.vector
        def _(dve):
            steps = [0]

            def settle(ins):
                steps[0] += 1
                ins.then_inc(dve_step, 1)
                dve.wait_ge(dve_step, steps[0])

            lns = [0]

            def normalize(dst, src, ready, done, first):
                n = lns[0]
                lns[0] += 1
                for k in range(TT):
                    ins = nc.vector.bn_stats(stats[:, k, :], src[:, k, :])
                settle(ins)
                for k in range(TT):
                    ins = nc.vector.bn_aggr(mean_var[:, n % 2, k, :], stats[:, k, :])
                ins.then_inc(ready, 1)
                dve.wait_ge(done, n - first + 1)
                for k in range(TT):
                    ins = nc.vector.tensor_scalar(dst[:, k, :], src[:, k, :], mean_var[:, n % 2, k, 0:1],
                                                  rstd[:, n % 2, k:k + 1], ALU.subtract, ALU.mult)
                return ins

            def take(name, c):
                n = FIRST_N[name, c]
                dve.wait_ge(job_full, n + 1)
                return n % 4

            def mix(x_shifted, xr, xk, ready):
                for dst, mu in ((xr, "mu_r"), (xk, "mu_k")):
                    for k in range(CT):
                        ins = nc.vector.tensor_scalar(dst[:, k], x_shifted[:, k, 1:], cols[:, COL[mu], k:k + 1],
                                                      None, ALU.mult)
                settle(ins)
                for dst, om in ((xr, "om_r"), (xk, "om_k")):
                    for k in range(CT):
                        ins = nc.vector.scalar_tensor_tensor(
                            out=dst[:, k], in0=x_shifted[:, k, 0:CHUNK], scalar=cols[:, COL[om], k:k + 1],
                            in1=dst[:, k], op0=ALU.mult, op1=ALU.add)
                ins.then_inc(ready, 1)

            def over_tokens(v):
                return v[:].rearrange("p (a d) -> p a d", a=1).to_broadcast([P, TT, DIM])

            dve.wait_ge(x_loaded[0], 16)
            normalize(a_xn1[0], a_x[0], stats_ready, rstd_ready, 0).then_inc(xn1_ready, 1)
            dve.wait_ge(rest_loaded, 16 * 15)
            for src, dst in (("mu_r", "om_r"), ("mu_k", "om_k")):
                ins = nc.vector.tensor_scalar(cols[:, COL[dst], :], cols[:, COL[src], :], -1.0, 1.0,
                                              ALU.mult, ALU.add)
            settle(ins)

            for t in range(CHUNKS + 2):
                a, b, c = t, t - 1, t - 2
                if 0 <= b < CHUNKS:
                    n = take("yT", b)
                    if b >= 2:
                        dve.wait_ge(x2_stored, 16 * (b - 1))
                    x1 = a_x1[b % 2]
                    ins = nc.vector.tensor_tensor(x1, a_xn1[b % 2], slot_tok(n), ALU.add)
                    ins.then_inc(z_ready, 1)
                    dve.wait_ge(z_ready, b + 1)
                    settle(normalize(x1, x1, stats_ready, rstd_ready, 0))
                    settle(nc.vector.tensor_tensor(x1, x1, over_tokens(gamma_b), ALU.mult))
                    settle(nc.vector.tensor_tensor(x1, x1, over_tokens(beta_b), ALU.add))
                    nc.vector.tensor_tensor(x1, x1, a_x[b % 3], ALU.add).then_inc(x1_ready, 1)
                    dve.wait_ge(x1_ready, b + 1)
                    normalize(a_xn2, x1, stats_ready, rstd_ready, 0).then_inc(xn2_ready, 1)
                if 0 <= c < CHUNKS:
                    n = take("kv", c)
                    nc.vector.tensor_tensor(a_r, a_r, slot_tok(n), ALU.mult).then_inc(rkv_ready, 1)
                    dve.wait_ge(rkv_ready, c + 1)
                    x2 = a_x1[c % 2]
                    nc.vector.tensor_tensor(x2, x2, a_r, ALU.add).then_inc(x2_ready, 1)
                    dve.wait_ge(x2_ready, c + 1)
                    normalize(a_xn3, x2, stats_ready, rstd_ready, 0).then_inc(xn3_ready, 1)
                if a < CHUNKS:
                    dve.wait_ge(f_ready, a + 1)
                    dve.wait_ge(is_ready, a + 1)
                    for k in range(CT):
                        before = a_h[(a + 1) % 2][:, k, CHUNK - 1:CHUNK] if a else 0.0
                        ins = nc.vector.tensor_tensor_scan(a_h[a % 2][:, k], a_f[:, k], a_i[:, k], before,
                                                           ALU.mult, ALU.add)
                    ins.then_inc(h_ready, 1)
                if 0 <= b < CHUNKS:
                    dve.wait_ge(x2T_ready, b + 1)
                    if b == 0:
                        dve.wait_ge(consts_ready, 5)
                    mix(a_x2T[b % 2], a_xr, a_xk, mix_ready)
                if 0 <= c < CHUNKS:
                    for m, (full, parts) in enumerate(((a_qf, a_qp), (a_kf, a_kp))):
                        dve.wait_ge(part0_ready, 2 * c + m + 1)
                        nc.vector.tensor_tensor(full, full, parts[:, 0], ALU.subtract).then_inc(rest1_ready, 1)
                    n = take("v", c)
                    if c == 0:
                        dve.wait_ge(consts_ready, 5)
                    nc.vector.tensor_tensor(
                        v_aug[:, c * TT:(c + 1) * TT, :, 0:HD],
                        slot_tok(n).rearrange("p t (h d) -> p t h d", d=HD),
                        bv_b[:].rearrange("p (a h d) -> p a h d", a=1, d=HD).to_broadcast([P, TT, HEADS, HD]),
                        ALU.add).then_inc(v_ready, 1)
                if t + 1 < CHUNKS:
                    dve.wait_ge(x_loaded[(t + 1) % 3], 16 * ((t + 1) // 3 + 1))
                    normalize(a_xn1[(t + 1) % 2], a_x[(t + 1) % 3], stats_ready, rstd_ready, 0)\
                        .then_inc(xn1_ready, 1)
            first_lns = lns[0]
            barrier(dve, phase_a_done)

            nc.vector.memset(pv_bank, 0.0).then_inc(pv_cleared, 1)
            jobs = reduced = 0
            for item in ORDER:
                if item[0] == "max":
                    _, s, qt, h, k0, k1 = item
                    dve.wait_ge(m_full, jobs + 1)
                    nc.vector.tensor_reduce(span_max[:, s % 2, qt * HG + h, k0 // SPAN:k0 // SPAN + 1],
                                            slot(jobs % 2)[:, 0:k1 - k0], AX.X, ALU.max)\
                        .then_inc(span_reduced, 1)
                    jobs += 1
                    reduced += 1
                    if qt == TT - 1 and h == HG - 1 and k1 == (STEPS[s][1] + 1) * CHUNK:
                        dve.wait_ge(span_reduced, reduced)
                        spans = (k1 + SPAN - 1) // SPAN
                        nm, parts = neg_max, shift_parts[:, s % 2]
                        settle(nc.vector.tensor_reduce(nm[:, 0], span_max[:, s % 2, :, 0:spans], AX.X, ALU.max,
                                                       negate=True))
                        settle(nc.vector.tensor_copy(parts[:, :, 0], nm[:, 0]))
                        settle(nc.vector.tensor_tensor(nm[:, 1], nm[:, 0], parts[:, :, 0], ALU.subtract))
                        settle(nc.vector.tensor_copy(parts[:, :, 1], nm[:, 1]))
                        settle(nc.vector.tensor_tensor(nm[:, 2], nm[:, 1], parts[:, :, 1], ALU.subtract))
                        nc.vector.tensor_copy(parts[:, :, 2], nm[:, 2]).then_inc(shift_ready, 1)
                elif item[0] == "shift":
                    jobs += 1
                elif item[0] == "out":
                    s = item[1]
                    g, c = STEPS[s]
                    dve.wait_ge(m_full, jobs + 1)
                    o = slot(jobs % 2)[:, 0:CHUNK].rearrange("p (t h d) -> p t h d", t=TT, h=HG)
                    settle(nc.vector.reciprocal(inv_sum[:, s % 2], o[:, :, :, HD]))
                    nc.vector.tensor_tensor(
                        attn[:, c * TT:(c + 1) * TT, g * HG * HD:(g + 1) * HG * HD].rearrange(
                            "p t (h d) -> p t h d", d=HD),
                        o[:, :, :, 0:HD],
                        inv_sum[:, s % 2].rearrange("p t (h a) -> p t h a", a=1).to_broadcast([P, TT, HG, HD]),
                        ALU.mult).then_inc(attn_ready, 1)
                    jobs += 1
            barrier(dve, phase_b_done)

            def c_take(name, c):
                n = LAST_N[name, c]
                dve.wait_ge(c_full, n + 1)
                return n % 4

            for t in range(CHUNKS + 2):
                a, b, c = t, t - 1, t - 2
                if 0 <= b < CHUNKS:
                    dve.wait_ge(x4T_ready, b + 1)
                    if b == 0:
                        dve.wait_ge(consts_ready, 6)
                    mix(c_x4T[b % 2], c_xr, c_xk, c_mix)
                if 0 <= c < CHUNKS:
                    n = c_take("kv", c)
                    nc.vector.tensor_tensor(c_r, c_r, slot_tok(n), ALU.mult).then_inc(c_rkv, 1)
                    dve.wait_ge(c_rkv, c + 1)
                    nc.vector.tensor_tensor(c_x[c % 4], c_x[c % 4], c_r, ALU.add).then_inc(c_out, 1)
                if a < CHUNKS:
                    x3 = c_x[a % 4]
                    dve.wait_ge(c_loaded[a % 4], 16 * (a // 4 + 1))
                    settle(nc.vector.tensor_tensor(x3, x3, over_tokens(bo_b), ALU.add))
                    n = c_take("proj", a)
                    nc.vector.tensor_tensor(x3, x3, slot_tok(n), ALU.add).then_inc(c_x3, 1)
                    dve.wait_ge(c_x3, a + 1)
                    normalize(c_xn4, x3, c_stats, c_rstd, first_lns).then_inc(xn4_ready, 1)

        @block.tensor
        def _(pe):
            FIRST_READ = {"yT": z_ready, "r": r_ready, "k": relu_ready, "x1T": x1T_ready, "kv": rkv_ready,
                          "f": f_ready, "i": i_ready, "s": s_ready, "o": o_ready, "x3T": x3T_ready,
                          "x2T": x2T_ready, "q": part0_ready, "kk": part0_ready, "v": v_ready}
            LAST_READ = {"x4T": x4T_ready, "aT": aT_ready, "kv": c_rkv, "proj": c_x3, "r": c_r_ready,
                         "k": c_relu}

            def claim(m, jobs, read):
                if m >= 4:
                    name, c = jobs[m - 4]
                    pe.wait_ge(read[name], {"q": 2 * c + 1, "kk": 2 * c + 2}.get(name, c + 1))
                return m % 4

            def to_channels(n, src):
                for k in range(CT):
                    for j in range(TT):
                        ins = nc.tensor.transpose(slot_chan(n)[:, k, j * P:(j + 1) * P],
                                                  src[:, j, k * P:(k + 1) * P], ident[:])
                return ins

            def channels_out(n, w, src):
                for e in range(CT):
                    for k in range(CT):
                        ins = nc.tensor.matmul(slot_chan(n)[:, e], w[:, k, e * P:(e + 1) * P], src[:, k],
                                               start=(k == 0), stop=(k == CT - 1))
                return ins

            def tokens_out(n, w, src):
                for j in range(TT):
                    for k in range(CT):
                        ins = nc.tensor.matmul(slot_tok(n)[:, j], src[:, k, j * P:(j + 1) * P], w[:, k],
                                               start=(k == 0), stop=(k == CT - 1))
                return ins

            pe.wait_ge(consts_ready, 3)
            for m, (name, c) in enumerate(FIRST):
                n = claim(m, FIRST, FIRST_READ)
                if name == "yT":
                    pe.wait_ge(y_ready, c + 1)
                    for j in range(TT):
                        for k in range(CT):
                            ins = nc.tensor.transpose(slot_tok(n)[:, j, k * P:(k + 1) * P],
                                                      a_o[:, k, j * P:(j + 1) * P], ident[:])
                elif name == "r":
                    pe.wait_ge(mix_ready, c + 1)
                    if c == 0:
                        pe.wait_ge(rest_loaded, 16 * 15)
                    ins = tokens_out(n, weights["r"], a_xr)
                elif name == "k":
                    ins = channels_out(n, weights["k"], a_xk)
                elif name == "x1T":
                    pe.wait_ge(xn1_ready, c + 1)
                    ins = to_channels(n, a_xn1[c % 2])
                elif name == "kv":
                    pe.wait_ge(k2_ready, c + 1)
                    ins = tokens_out(n, weights["v"], a_k)
                elif name in ("f", "i", "s", "o"):
                    if name == "f":
                        pe.wait_ge(x1T_ready, c + 1)
                        pe.wait_ge(gates_loaded, 16 * 8)
                    ins = channels_out(n, weights[name], a_x1T)
                elif name == "x3T":
                    pe.wait_ge(xn3_ready, c + 1)
                    ins = to_channels(n, a_xn3)
                elif name == "x2T":
                    pe.wait_ge(xn2_ready, c + 1)
                    ins = to_channels(n, a_xn2)
                elif name == "q":
                    pe.wait_ge(x3T_ready, c + 1)
                    ins = channels_out(n, weights["aq"], a_x3T)
                elif name == "kk":
                    ins = channels_out(n, weights["ak"], a_x3T)
                elif name == "v":
                    ins = tokens_out(n, weights["av"], a_x3T)
                ins.then_inc(job_full, 1)
            barrier(pe, phase_a_done)

            scores = 0
            q_seen, k_seen = -1, -1

            reads = []
            spans_sent = 0

            def claim_m(read, value):
                if len(reads) >= 2:
                    pe.wait_ge(*reads[-2])
                reads.append((read, value))
                return (len(reads) - 1) % 2

            for item in ORDER:
                if item[0] == "max":
                    _, s, qt, h, k0, k1 = item
                    g, c = STEPS[s]
                    spans_sent += 1
                    n = claim_m(span_reduced, spans_sent)
                    if s != q_seen:
                        q_seen = s
                        pe.wait_ge(q_loaded[s % 3], 16 * len(Q_PARTS) * (s // 3 + 1))
                    if (g, c > 0) != k_seen:
                        k_seen = (g, c > 0)
                        if g == 0:
                            pe.wait_ge(k_loaded[c > 0], 16 * len(K_PARTS) + 16 * (CHUNKS - 1 if c > 0 else 1))
                        elif g == 1:
                            pe.wait_ge(k_loaded[2], 16 * len(K_PARTS) + 16 * CHUNKS)
                        else:
                            pe.wait_ge(k_loaded[g % 2], 16 * len(K_PARTS) * 2 + 16 * (CHUNKS - 1 if g % 2 else 1))
                    for a in range(k0, k1, CHUNK):
                        b = min(a + CHUNK, k1)
                        ends = b == (c * TT + qt + 1) * P
                        ins = nc.tensor.matmul(slot(n)[:, a - k0:b - k0],
                                               q_stack[0:SCORE_ROWS, s % 3, h, qt * P:(qt + 1) * P],
                                               k_stack[0:SCORE_ROWS, g % 2, h, a:b], start=True, stop=not ends)
                        if ends:
                            ins = nc.tensor.matmul(slot(n)[:, b - P - k0:b - k0], ident_b[:], mask_b[:],
                                                   start=False, stop=True)
                    ins.then_inc(m_full, 1)
                elif item[0] == "shift":
                    s = item[1]
                    n = claim_m(shift_placed, s + 1)
                    pe.wait_ge(shift_ready, s + 1)
                    for qt in range(TT):
                        ins = nc.tensor.matmul(
                            slot(n)[SCORE_ROWS:STACK, qt * P:(qt + 1) * P],
                            shift_parts[:, s % 2, qt * HG:(qt + 1) * HG, :].rearrange("p h r -> p (h r)"),
                            ident_b[:], start=True, stop=True)
                    ins.then_inc(m_full, 1)
                elif item[0] == "scores":
                    _, s, j, tile, half = item
                    g, c = STEPS[s]
                    q0 = max(0, j - c * TT) * P
                    if j == 0 and half == 0:
                        pe.wait_ge(shift_placed, s + 1)
                    for h in range(half * 2, half * 2 + 2):
                        if scores >= SCORE_RING:
                            pe.wait_ge(exp_done, scores - SCORE_RING + 1)
                        ins = nc.tensor.matmul(score_bank[scores % SCORE_RING][:, q0:],
                                               k_stack[0:STACK, g % 2, h, j * P:(j + 1) * P],
                                               q_stack[0:STACK, s % 3, h, q0:], start=True, stop=True)
                        ins.then_inc(scored, 1)
                        scores += 1
                elif item[0] == "pv":
                    tile = item[1]
                    s = next(k for k, e in enumerate(last_tile) if tile < e)
                    g, c = STEPS[s]
                    j = tile - (last_tile[s] - TT * (c + 1))
                    d = j - c * TT
                    if d >= 0:
                        pe.wait_ge(masked, s * TT + d + 1)
                    else:
                        pe.wait_ge(exp_done, HG * (tile + 1))
                    if j == 0:
                        if s == 0:
                            pe.wait_ge(pv_cleared, 1)
                        else:
                            pe.wait_ge(o_copied, s)
                    q0 = max(0, d) * P
                    for h in range(HG):
                        ins = nc.tensor.matmul(pv_bank[32 * h:32 * h + VW, q0:], v_aug[:, j, g * HG + h, :],
                                               probs[:, tile % 3, h, q0:], start=(j == 0),
                                               stop=(j == TT * (c + 1) - 1))
                    ins.then_inc(pv_done, 1)
                elif item[0] == "out":
                    s = item[1]
                    n = claim_m(attn_ready, s + 1)
                    pe.wait_ge(o_copied, s + 1)
                    for qt in range(TT):
                        ins = nc.tensor.transpose(slot(n)[:, qt * P:(qt + 1) * P],
                                                  oT[:, s % 2, qt * P:(qt + 1) * P], ident[:])
                    ins.then_inc(m_full, 1)
            barrier(pe, phase_b_done)

            for m, (name, c) in enumerate(LAST):
                n = claim(m, LAST, LAST_READ)
                if name == "x4T":
                    pe.wait_ge(xn4_ready, c + 1)
                    ins = to_channels(n, c_xn4)
                elif name == "aT":
                    ins = to_channels(n, attn[:, c * TT:(c + 1) * TT, :])
                elif name == "kv":
                    pe.wait_ge(c_k2, c + 1)
                    ins = tokens_out(n, weights["v"], c_k)
                elif name == "proj":
                    pe.wait_ge(aT_ready, c + 1)
                    ins = tokens_out(n, weights["ao"], c_aT)
                elif name == "r":
                    pe.wait_ge(c_mix, c + 1)
                    ins = tokens_out(n, weights["r"], c_xr)
                elif name == "k":
                    ins = channels_out(n, weights["k"], c_xk)
                ins.then_inc(c_full, 1)


_INS = ["x", "Wi", "bi", "Wf", "bf", "Wo_gate", "bo_gate", "Ws", "bs", "gamma", "beta", "WqT", "bq", "WkT", "bk",
        "WvT", "bv", "WoT", "bo", "WrT", "WkfT", "WvfT", "mu_r", "mu_k"]


def kernel(L0_attn_a_x, L0_attn_a_Wi, L0_attn_a_bi, L0_attn_a_Wf, L0_attn_a_bf, L0_attn_a_Wo, L0_attn_a_bo,
           L0_attn_a_Ws, L0_attn_a_bs, L0_attn_a_gamma, L0_attn_a_beta, L0_attn_b_Wq, L0_attn_b_bq, L0_attn_b_Wk,
           L0_attn_b_bk, L0_attn_b_Wv, L0_attn_b_bv, L0_attn_b_Wo, L0_attn_b_bo, L0_ffn_W_r, L0_ffn_W_k,
           L0_ffn_W_v, L0_ffn_mu_r, L0_ffn_mu_k):
    from concourse import bacc
    from concourse.bass_utils import run_bass_kernel_spmd

    given = [L0_attn_a_x.reshape(TOKENS, DIM), L0_attn_a_Wi, L0_attn_a_bi, L0_attn_a_Wf, L0_attn_a_bf,
             L0_attn_a_Wo, L0_attn_a_bo, L0_attn_a_Ws, L0_attn_a_bs, L0_attn_a_gamma, L0_attn_a_beta,
             L0_attn_b_Wq.T, L0_attn_b_bq, L0_attn_b_Wk.T, L0_attn_b_bk, L0_attn_b_Wv.T, L0_attn_b_bv,
             L0_attn_b_Wo.T, L0_attn_b_bo, L0_ffn_W_r.T, L0_ffn_W_k.T, L0_ffn_W_v.T, L0_ffn_mu_r, L0_ffn_mu_k]
    nc = bacc.Bacc("TRN2", target_bir_lowering=False, num_devices=1)
    arrays, args = {}, []
    for name, a in zip(_INS, given):
        a = np.ascontiguousarray(a)
        arrays[f"in_{name}"] = a
        args.append(nc.dram_tensor(f"in_{name}", a.shape, mybir.dt.from_np(a.dtype), kind="ExternalInput").ap())
    out = nc.dram_tensor("out", (TOKENS, DIM), F32, kind="ExternalOutput").ap()
    build(nc, *args, out)
    result = run_bass_kernel_spmd(nc, [arrays], core_ids=[0])
    return result.results[0]["out"].reshape(1, TOKENS, DIM)
```

```python
from contextlib import ExitStack

import numpy as np

import concourse.bass as bass
from concourse import mybir

F32 = mybir.dt.float32
BF16 = mybir.dt.bfloat16
ALU = mybir.AluOpType
ACT = mybir.ActivationFunctionType
AX = mybir.AxisListType

P = 128
TOKENS, DIM = 4096, 256
CHUNK = 512
CHUNKS = TOKENS // CHUNK
TT = CHUNK // P
CT = DIM // P
HEADS, HD = 16, 16
HG = 4
GROUPS = HEADS // HG
EPS = 1e-5
SCALE = HD ** -0.5
MASKED = -1e30
SLOT = CT * CHUNK

Q_PARTS = (0, 0, 1, 0, 2, 1)
K_PARTS = (0, 1, 0, 2, 0, 1)
SCORE_ROWS = HD * len(Q_PARTS)
MAX_ROWS = 3 * HG
STACK = SCORE_ROWS + MAX_ROWS
VW = HD + 1
SHIFT_AHEAD = 1
SEEN, FREED = 230, 150
MASKING = 900
WORTH = 500
RANK = ["scores", "pv", "max"]
Q_RING = 4
SPAN = 1024
AHEAD = 8 * SPAN

STEPS = [(g, c if g % 2 == 0 else CHUNKS - 1 - c) for g in range(GROUPS) for c in range(CHUNKS)]


def first_jobs():
    order = []
    for t in range(CHUNKS + 2):
        for name, c in (("yT", t - 1), ("r", t - 2), ("k", t - 2), ("x1T", t), ("kv", t - 2), ("f", t), ("i", t),
                        ("s", t), ("o", t), ("x3T", t - 2), ("x2T", t - 1), ("q", t - 2), ("kk", t - 2),
                        ("v", t - 2)):
            if 0 <= c < CHUNKS:
                order.append((name, c))
    return order


def last_jobs():
    order = []
    for t in range(CHUNKS + 2):
        for name, c in (("x4T", t - 1), ("aT", t), ("kv", t - 2), ("proj", t), ("r", t - 1), ("k", t - 1)):
            if 0 <= c < CHUNKS:
                order.append((name, c))
    return order


def attention_order():
    def pe_ns(n):
        return 3 + n / 2.4

    def act_ns(n):
        return 50 + n / 1.2

    def dve_ns(n):
        return 64 + n / 0.96

    maxima = []
    for s, (g, c) in enumerate(STEPS):
        for qt in range(TT):
            for h in range(HG):
                keys = (c * TT + qt + 1) * P
                for a in range(0, keys, SPAN):
                    maxima.append((s, qt, h, a, min(a + SPAN, keys)))
    widths = [m[4] - m[3] for m in maxima]
    upto = [sum(1 for m in maxima if m[0] <= s) for s in range(len(STEPS))]
    work = [sum(widths[:n]) for n in upto]
    tiles = [(s, j) for s, (g, c) in enumerate(STEPS) for j in range(TT * (c + 1))]
    order = []
    pe = act = dve = 0.0
    slot_free, bank_free = [0.0, 0.0], [0.0, 0.0, 0.0]
    shift_at, placed_at, exp_at, copied_at = {}, {}, {}, {}
    jobs = scored = summed = made = 0
    made_work = 0
    shifted = outs = 0

    def job(cost):
        nonlocal pe, jobs
        pe = max(pe, slot_free[jobs % 2]) + cost
        jobs += 1
        return pe + SEEN

    while summed < len(tiles) or outs < len(STEPS):
        s_now = tiles[scored // HG][0] if scored < HG * len(tiles) else len(STEPS) - 1
        can = {}
        if made < upto[min(s_now + Q_RING - 1, len(STEPS) - 1)]:
            can["max"] = slot_free[jobs % 2]
        if shifted < len(STEPS) and made >= upto[shifted] and shifted <= s_now + SHIFT_AHEAD:
            can["shift"] = max(slot_free[jobs % 2], shift_at[shifted] + FREED)
        if scored < HG * len(tiles) and tiles[scored // HG][0] in placed_at:
            if scored // HG < summed + 3:
                can["scores"] = max(bank_free[scored % 3], placed_at[tiles[scored // HG][0]])
        if summed < len(tiles) and scored >= HG * (summed + 1):
            s, j = tiles[summed]
            can["pv"] = exp_at[summed] + FREED
            if j == 0 and s:
                can["pv"] = max(can["pv"], copied_at[s - 1] + FREED)
        if outs in copied_at:
            can["out"] = max(slot_free[jobs % 2], copied_at[outs] + FREED)
        s, j = tiles[min(scored // HG, len(tiles) - 1)]
        whole = TT * (STEPS[s][1] + 1)
        after = min(s + 1, len(STEPS) - 1)
        due = work[s] + (work[after] - work[s]) * (j + 1) / whole + AHEAD
        late = made_work < due
        rank = ["shift", "out"] + (["max", "pv", "scores"] if late else RANK)
        ready = [k for k in rank if k in can and can[k] <= pe]
        kind = ready[0] if ready else min((k for k in rank if k in can), key=lambda k: can[k])
        if kind == "pv" and late and "max" in can and can["max"] <= pe + WORTH:
            kind = "scores" if "scores" in ready else "max"
        if kind == "max":
            m = maxima[made]
            seen = job(pe_ns(widths[made]) + 60)
            dve = max(dve, seen) + dve_ns(widths[made])
            slot_free[(jobs - 1) % 2] = dve + FREED
            order.append(("max", *m))
            made_work += widths[made]
            made += 1
            if made in upto:
                dve += 1500
                shift_at[upto.index(made)] = dve
        elif kind == "shift":
            pe = max(pe, can["shift"])
            seen = job(240)
            act = max(act, seen) + HG * act_ns(CHUNK)
            slot_free[(jobs - 1) % 2] = act + FREED
            placed_at[shifted] = act + FREED
            order.append(("shift", shifted))
            shifted += 1
        elif kind == "scores":
            s, j = tiles[scored // HG]
            n = CHUNK - max(0, j - STEPS[s][1] * TT) * P
            pe = max(pe, can["scores"]) + pe_ns(n)
            order.append(("scores", s, j, scored // HG, scored % HG))
            act = max(act, pe + SEEN) + act_ns(n)
            bank_free[scored % 3] = act + FREED
            exp_at[scored // HG] = act + (MASKING if n < CHUNK or j == STEPS[s][1] * TT else 0)
            scored += 1
        elif kind == "pv":
            s, j = tiles[summed]
            n = CHUNK - max(0, j - STEPS[s][1] * TT) * P
            pe = max(pe, can["pv"]) + 4 * pe_ns(n)
            order.append(("pv", summed))
            summed += 1
            if j == TT * (STEPS[s][1] + 1) - 1:
                act = max(act, pe + SEEN) + act_ns(CHUNK)
                copied_at[s] = act
        else:
            pe = max(pe, can["out"])
            seen = job(4 * 56)
            dve = max(dve, seen) + 700
            slot_free[(jobs - 1) % 2] = dve + FREED
            order.append(("out", outs))
            outs += 1
    return order


def build(nc, x, Wi, bi, Wf, bf, Wo_gate, bo_gate, Ws, bs, gamma, beta, WqT, bq, WkT, bk, WvT, bv, WoT, bo,
          WrT, WkfT, WvfT, mu_r, mu_k, out):
    with ExitStack() as ctx:
        def sb(name, shape, dt=F32):
            return ctx.enter_context(nc.sbuf_tensor(name, shape, dt))

        def sem(name):
            return ctx.enter_context(nc.semaphore(name))

        weights = {n: sb("w_" + n, [P, CT, DIM]) for n in
                   ("f", "i", "s", "o", "r", "k", "v", "aq", "ak", "av", "ao")}
        gamma_b, beta_b, bv_b, bo_b = (sb(n, [P, DIM]) for n in ("gamma_b", "beta_b", "bv_b", "bo_b"))
        cols = sb("cols", [P, 10, CT])
        COL = {n: k for k, n in enumerate(("f", "i", "s", "o", "aq", "ak", "mu_r", "mu_k", "om_r", "om_k"))}
        ident = sb("ident", [P, P])
        ident_b = sb("ident_b", [P, P], BF16)
        mask_b = sb("mask_b", [P, P], BF16)
        v_aug = sb("v_aug", [P, TOKENS // P, HEADS, VW])
        q_stack = sb("q_stack", [P, Q_RING, HG, CHUNK], BF16)
        head_rows = sb("head_rows", [P, HG, CHUNK], BF16)
        stats = sb("stats", [P, TT, 6])
        mean_var = sb("mean_var", [P, 2, TT, 2])
        var_eps = sb("var_eps", [P, 2, TT])
        rstd = sb("rstd", [P, 2, TT])
        minus_half = sb("minus_half", [P, TT])
        span_max = sb("span_max", [P, 2, TT * HG, TOKENS // SPAN])
        neg_max = sb("neg_max", [P, 3, TT * HG])
        shift_parts = sb("shift_parts", [P, 2, TT * HG, 3], BF16)
        inv_sum = sb("inv_sum", [P, 2, TT, HG])

        BLK = TT * DIM
        arena = sb("arena", [P, 31 * BLK + 8])

        def blk(n, k=1):
            return arena[:, n * BLK:(n + k) * BLK]

        def tok(n):
            return blk(n).rearrange("p (t d) -> p t d", t=TT)

        def chan(n):
            return blk(n).rearrange("p (k t) -> p k t", k=CT)

        a_x = [tok(n) for n in (0, 1, 2)]
        a_xn1 = [tok(n) for n in (3, 4)]
        a_x1T = chan(5)
        a_f, a_i, a_s, a_o = (chan(n) for n in (6, 7, 8, 9))
        a_h = [chan(n) for n in (10, 11)]
        a_x1 = [tok(n) for n in (12, 13)]
        a_xn2, a_xn3 = tok(14), tok(15)
        a_xr, a_xk, a_x3T, a_k = (chan(n) for n in (16, 17, 18, 19))
        a_r = tok(20)
        a_qf, a_kf = chan(21), chan(22)
        a_qp, a_kp = (arena[:, n * BLK:n * BLK + 3 * BLK // 2].bitcast(BF16).rearrange(
            "p (r k t) -> p r k t", r=3, k=CT) for n in (23, 25))
        WT = CHUNK + 1
        a_x2T = [arena[:, 27 * BLK + b * CT * WT:27 * BLK + (b + 1) * CT * WT].rearrange(
            "p (k t) -> p k t", k=CT) for b in range(2)]
        k_stack = blk(0, 16).bitcast(BF16).rearrange("p (b h t) -> p b h t", b=2, h=HG)
        probs = blk(16, 6).rearrange("p (b h t) -> p b h t", b=3, h=HG)
        oT = blk(22).rearrange("p (b t) -> p b t", b=2)
        attn = blk(23, 8).rearrange("p (t d) -> p t d", d=DIM)
        c_x = [tok(n) for n in (0, 1, 2, 3)]
        c_aT, c_xr, c_xk, c_k = (chan(n) for n in (4, 5, 6, 7))
        c_r, c_xn4 = tok(8), tok(9)
        c_x4T = [arena[:, 10 * BLK + b * CT * WT:10 * BLK + (b + 1) * CT * WT].rearrange(
            "p (k t) -> p k t", k=CT) for b in range(2)]

        psum = ctx.enter_context(nc.psum_tensor("psum", [P, 4 * SLOT], F32))

        def slot(n):
            return psum[:, n * SLOT:(n + 1) * SLOT]

        def slot_chan(n):
            return slot(n).rearrange("p (k t) -> p k t", k=CT)

        def slot_tok(n):
            return slot(n).rearrange("p (t d) -> p t d", t=TT)

        SCORE_RING = 3
        score_bank = [psum[:, 2 * SLOT + b * CHUNK:2 * SLOT + (b + 1) * CHUNK] for b in range(SCORE_RING)]
        pv_bank = psum[:, 2 * SLOT + 3 * CHUNK:4 * SLOT]

        q_dram = nc.dram_tensor("q_parts", (3, DIM, TOKENS), BF16, kind="Internal").ap()
        k_dram = nc.dram_tensor("k_parts", (3, DIM, TOKENS), BF16, kind="Internal").ap()
        x2_dram = nc.dram_tensor("x2_rows", (TOKENS, DIM), F32, kind="Internal").ap()

        gates_loaded, rest_loaded = sem("gates_loaded"), sem("rest_loaded")
        x_loaded = [sem(f"x_loaded{b}") for b in range(3)]
        consts_ready = sem("consts_ready")
        job_full = sem("job_full")
        z_ready, i_ready, rkv_ready = sem("z_ready"), sem("i_ready"), sem("rkv_ready")
        dve_step, pool_step = sem("dve_step"), sem("pool_step")
        stats_ready, rstd_ready = sem("stats_ready"), sem("rstd_ready")
        xn1_ready, x1T_ready = sem("xn1_ready"), sem("x1T_ready")
        f_ready, s_ready, o_ready = sem("f_ready"), sem("s_ready"), sem("o_ready")
        is_ready, h_ready, y_ready = sem("is_ready"), sem("h_ready"), sem("y_ready")
        x1_ready, xn2_ready, x2T_ready = sem("x1_ready"), sem("xn2_ready"), sem("x2T_ready")
        mix_ready, r_ready, relu_ready, k2_ready = (sem(n) for n in ("mix_ready", "r_ready", "relu_ready",
                                                                     "k2_ready"))
        x2_ready, x2_stored, xn3_ready, x3T_ready = (sem(n) for n in ("x2_ready", "x2_stored", "xn3_ready",
                                                                      "x3T_ready"))
        part0_ready, rest1_ready, part1_ready, part2_ready = (sem(n) for n in (
            "part0_ready", "rest1_ready", "part1_ready", "part2_ready"))
        parts_stored, v_ready = sem("parts_stored"), sem("v_ready")
        phase_a_done, pv_cleared = sem("phase_a_done"), sem("pv_cleared")
        k_loaded = [sem(f"k_loaded{b}") for b in range(4)]
        q_loaded = [sem(f"q_loaded{b}") for b in range(Q_RING)]
        m_full = sem("m_full")
        span_reduced, attn_ready = sem("span_reduced"), sem("attn_ready")
        scored, exp_done, masked, pv_done = sem("scored"), sem("exp_done"), sem("masked"), sem("pv_done")
        shift_ready, shift_placed = sem("shift_ready"), sem("shift_placed")
        o_copied = sem("o_copied")
        c_loaded = [sem(f"c_loaded{b}") for b in range(4)]
        aT_ready, xn4_ready, x4T_ready = sem("aT_ready"), sem("xn4_ready"), sem("x4T_ready")
        c_mix, c_r_ready, c_relu, c_k2 = sem("c_mix"), sem("c_r_ready"), sem("c_relu"), sem("c_k2")
        c_out, stored = sem("c_out"), sem("stored")
        c_stats, c_rstd = sem("c_stats"), sem("c_rstd")
        c_full = sem("c_full")
        c_rkv, c_x3 = sem("c_rkv"), sem("c_x3")

        block = ctx.enter_context(nc.Block())

        FIRST, LAST, ORDER = first_jobs(), last_jobs(), attention_order()
        FIRST_N = {job: n for n, job in enumerate(FIRST)}
        LAST_N = {job: n for n, job in enumerate(LAST)}
        last_tile = []
        for g, c in STEPS:
            last_tile.append((last_tile[-1] if last_tile else 0) + TT * (c + 1))

        def leave(eng):
            eng.drain().then_inc(phase_a_done, 1)

        def rows(dram, c):
            return dram[c * CHUNK:(c + 1) * CHUNK, :].rearrange("(t p) d -> p t d", p=P)

        @block.sync
        def _(sp):
            def load_x(c):
                if c >= 3:
                    sp.wait_ge(x1_ready, c - 2)
                sp.dma_start(a_x[c % 3], rows(x, c)).then_inc(x_loaded[c % 3], 16)

            def vector(dst, v, s):
                sp.dma_start(cols[:, COL[dst], :], v.rearrange("(k p) -> p k", p=P),
                             allow_slow_non_contiguous=True).then_inc(s, 16)

            def matrix(dst, w, s):
                sp.dma_start(weights[dst][:], w.rearrange("(k p) e -> p k e", p=P)).then_inc(s, 16)

            def load_k(g, b, c0, c1):
                for i, r in enumerate(K_PARTS):
                    src = k_dram[r, g * HG * HD:(g + 1) * HG * HD, c0 * CHUNK:c1 * CHUNK]
                    sp.dma_start(k_stack[HD * i:HD * (i + 1), g % 2, :, c0 * CHUNK:c1 * CHUNK],
                                 src.rearrange("(h d) t -> d h t", d=HD)).then_inc(k_loaded[b], 16)
                if g < 2:
                    for c in range(c0, c1):
                        sp.dma_start(k_stack[SCORE_ROWS:STACK, g % 2, :, c * CHUNK:(c + 1) * CHUNK],
                                     head_rows[SCORE_ROWS:STACK]).then_inc(k_loaded[b], 16)

            def load_q(s):
                g, c = STEPS[s]
                if s >= Q_RING:
                    sp.wait_ge(scored, HG * last_tile[s - Q_RING])
                for i, r in enumerate(Q_PARTS):
                    src = q_dram[r, g * HG * HD:(g + 1) * HG * HD, c * CHUNK:(c + 1) * CHUNK]
                    sp.dma_start(q_stack[HD * i:HD * (i + 1), s % Q_RING],
                                 src.rearrange("(h d) t -> d h t", d=HD)).then_inc(q_loaded[s % Q_RING], 16)

            load_x(0)
            for n, w, b in (("f", Wf, bf), ("i", Wi, bi), ("s", Ws, bs), ("o", Wo_gate, bo_gate)):
                matrix(n, w, gates_loaded)
                vector(n, b, gates_loaded)
            load_x(1)
            load_x(2)
            for n, w in (("r", WrT), ("k", WkfT), ("v", WvfT), ("aq", WqT), ("ak", WkT), ("av", WvT), ("ao", WoT)):
                matrix(n, w, rest_loaded)
            for n, v in (("aq", bq), ("ak", bk), ("mu_r", mu_r), ("mu_k", mu_k)):
                vector(n, v, rest_loaded)
            for dst, v in ((gamma_b, gamma), (beta_b, beta), (bv_b, bv), (bo_b, bo)):
                sp.dma_start(dst[:], v.partition_broadcast(P)).then_inc(rest_loaded, 16)
            for t in range(2, CHUNKS + 2):
                c = t - 2
                if t + 1 < CHUNKS:
                    load_x(t + 1)
                if c == CHUNKS - 1:
                    sp.wait_ge(x1_ready, CHUNKS)
                    sp.wait_ge(parts_stored, 6 * 16 * c)
                    load_k(0, 0, 0, 1)
                    load_q(0)
                    load_q(1)
                    load_k(0, 3, 1, CHUNKS - 1)
                    load_q(2)
                sp.wait_ge(x2_ready, c + 1)
                sp.dma_start(rows(x2_dram, c), a_x1[c % 2]).then_inc(x2_stored, 16)
                sp.wait_ge(part2_ready, 2 * (c + 1))
                for dram, parts in ((q_dram, a_qp), (k_dram, a_kp)):
                    for r in range(3):
                        sp.dma_start(dram[r, :, c * CHUNK:(c + 1) * CHUNK].rearrange("(k p) t -> p k t", p=P),
                                     parts[:, r]).then_inc(parts_stored, 16)
            leave(sp)
            sp.wait_ge(parts_stored, 6 * 16 * CHUNKS)
            sp.wait_ge(x2_stored, 16 * CHUNKS)
            load_k(0, 1, CHUNKS - 1, CHUNKS)
            for s in range(3, Q_RING):
                load_q(s)
            for s in range(len(STEPS)):
                if s % CHUNKS == 0 and s // CHUNKS + 1 < GROUPS:
                    if s:
                        sp.wait_ge(scored, HG * last_tile[s - 1])
                    else:
                        sp.wait_ge(phase_a_done, 5)
                    load_k(s // CHUNKS + 1, 2 if s == 0 else (s // CHUNKS + 1) % 2, 0, CHUNKS)
                if s + Q_RING < len(STEPS):
                    load_q(s + Q_RING)

            def load_c(c):
                if c >= 4:
                    sp.wait_ge(stored, 16 * (c - 3))
                sp.dma_start(c_x[c % 4], rows(x2_dram, c)).then_inc(c_loaded[c % 4], 16)

            sp.wait_ge(scored, HG * last_tile[-CHUNKS - 1])
            for c in range(4):
                load_c(c)
            for c in range(CHUNKS):
                sp.wait_ge(c_out, c + 1)
                sp.dma_start(rows(out, c), c_x[c % 4]).then_inc(stored, 16)
                if c + 4 < CHUNKS:
                    load_c(c + 4)
            sp.wait_ge(stored, 16 * CHUNKS)

        @block.gpsimd
        def _(pool):
            steps = [0]

            def settle(ins):
                steps[0] += 1
                ins.then_inc(pool_step, 1)
                pool.wait_ge(pool_step, steps[0])

            lns = [0]

            def rstd_of(ready, done, first):
                n = lns[0]
                lns[0] += 1
                pool.wait_ge(ready, n - first + 1)
                settle(nc.gpsimd.tensor_scalar(var_eps[:, n % 2, :], mean_var[:, n % 2, :, 1], EPS, None, ALU.add))
                nc.gpsimd.tensor_tensor(rstd[:, n % 2, :], var_eps[:, n % 2, :], minus_half[:],
                                        ALU.pow).then_inc(done, 1)

            settle(nc.gpsimd.memset(minus_half[:], -0.5))
            rstd_of(stats_ready, rstd_ready, 0)
            ready = [0]

            def const(ins):
                ready[0] += 1
                ins.then_inc(consts_ready, 1)
                pool.wait_ge(consts_ready, ready[0])

            for m in (ident, ident_b):
                settle(nc.gpsimd.memset(m[:], 0.0))
                const(nc.gpsimd.affine_select(out=m[:], in_=m[:], compare_op=ALU.not_equal, fill=1.0, base=0,
                                              pattern=[[-1, P]], channel_multiplier=1))
            settle(nc.gpsimd.memset(mask_b[:], 0.0))
            const(nc.gpsimd.affine_select(out=mask_b[:], in_=mask_b[:], compare_op=ALU.is_ge, fill=MASKED, base=0,
                                          pattern=[[-1, P]], channel_multiplier=1))
            settle(nc.gpsimd.memset(a_x2T[0][:, :, 0:1], 0.0))
            hr = head_rows[SCORE_ROWS:STACK]
            settle(nc.gpsimd.memset(hr, 1.0))
            settle(nc.gpsimd.affine_select(out=hr, in_=hr, compare_op=ALU.is_ge, fill=0.0, base=0,
                                           pattern=[[-3, HG], [0, CHUNK]], channel_multiplier=1))
            const(nc.gpsimd.affine_select(out=hr, in_=hr, compare_op=ALU.is_ge, fill=0.0, base=2,
                                          pattern=[[3, HG], [0, CHUNK]], channel_multiplier=-1))
            const(nc.gpsimd.memset(v_aug[:], 1.0))

            for t in range(CHUNKS + 2):
                if 0 <= t - 1 < CHUNKS:
                    rstd_of(stats_ready, rstd_ready, 0)
                    rstd_of(stats_ready, rstd_ready, 0)
                if 0 <= t - 2 < CHUNKS:
                    rstd_of(stats_ready, rstd_ready, 0)
                if t < CHUNKS:
                    pool.wait_ge(s_ready, t + 1)
                    nc.gpsimd.tensor_tensor(a_i[:], a_i[:], a_s[:], ALU.mult).then_inc(is_ready, 1)
                    pool.wait_ge(h_ready, t + 1)
                    pool.wait_ge(o_ready, t + 1)
                    nc.gpsimd.tensor_tensor(a_o[:], a_o[:], a_h[t % 2], ALU.mult).then_inc(y_ready, 1)
                if 0 <= t - 2 < CHUNKS:
                    for n, (rest, parts) in enumerate(((a_qf, a_qp), (a_kf, a_kp))):
                        pool.wait_ge(part1_ready, 2 * (t - 2) + n + 1)
                        nc.gpsimd.tensor_tensor(parts[:, 2], rest, parts[:, 1],
                                                ALU.subtract).then_inc(part2_ready, 1)
                if t + 1 < CHUNKS:
                    rstd_of(stats_ready, rstd_ready, 0)
            first_lns = lns[0]
            leave(pool)

            for item in ORDER:
                if item[0] == "scores" and item[4] == HG - 1:
                    _, s, j, tile, _ = item
                    g, c = STEPS[s]
                    d = j - c * TT
                    if d >= 0:
                        pool.wait_ge(exp_done, HG * (tile + 1))
                        tri = probs[:, tile % 3, :, d * P:(d + 1) * P]
                        nc.gpsimd.affine_select(out=tri, in_=tri, compare_op=ALU.is_ge, fill=0.0, base=0,
                                                pattern=[[0, HG], [1, P]],
                                                channel_multiplier=-1).then_inc(masked, 1)
            pool.wait_ge(c_full, 1)

            const(nc.gpsimd.memset(c_x4T[0][:, :, 0:1], 0.0))
            for t in range(CHUNKS):
                rstd_of(c_stats, c_rstd, first_lns)

        @block.scalar
        def _(act):
            def take(name, c):
                n = FIRST_N[name, c]
                act.wait_ge(job_full, n + 1)
                return n % 4

            for t in range(CHUNKS + 2):
                a, b, c = t, t - 1, t - 2
                if 0 <= c < CHUNKS:
                    n = take("r", c)
                    if c:
                        act.wait_ge(x2_ready, c)
                    act.activation(a_r, slot_tok(n), ACT.Sigmoid).then_inc(r_ready, 1)
                    n = take("k", c)
                    act.activation(a_k, slot_chan(n), ACT.Relu).then_inc(relu_ready, 1)
                    act.wait_ge(relu_ready, c + 1)
                    act.activation(a_k, a_k, ACT.Square).then_inc(k2_ready, 1)
                if a < CHUNKS:
                    n = take("x1T", a)
                    act.activation(a_x1T, slot_chan(n), ACT.Copy).then_inc(x1T_ready, 1)
                    if a:
                        act.wait_ge(h_ready, a)
                    n = take("f", a)
                    act.wait_ge(gates_loaded, 16 * 8)
                    for k in range(CT):
                        ins = act.activation(a_f[:, k], slot_chan(n)[:, k], ACT.Sigmoid,
                                             bias=cols[:, COL["f"], k:k + 1])
                    ins.then_inc(f_ready, 1)
                    n = take("i", a)
                    for k in range(CT):
                        ins = act.activation(a_i[:, k], slot_chan(n)[:, k], ACT.Sigmoid,
                                             bias=cols[:, COL["i"], k:k + 1])
                    ins.then_inc(i_ready, 1)
                    n = take("s", a)
                    for k in range(CT):
                        ins = act.activation(a_s[:, k], slot_chan(n)[:, k], ACT.Tanh,
                                             bias=cols[:, COL["s"], k:k + 1])
                    ins.then_inc(s_ready, 1)
                    n = take("o", a)
                    for k in range(CT):
                        ins = act.activation(a_o[:, k], slot_chan(n)[:, k], ACT.Sigmoid,
                                             bias=cols[:, COL["o"], k:k + 1])
                    ins.then_inc(o_ready, 1)
                if 0 <= c < CHUNKS:
                    n = take("x3T", c)
                    act.activation(a_x3T, slot_chan(n), ACT.Copy).then_inc(x3T_ready, 1)
                if 0 <= b < CHUNKS:
                    n = take("x2T", b)
                    if b:
                        act.wait_ge(mix_ready, b)
                    act.activation(a_x2T[(b + 1) % 2][:, :, 0:1], slot_chan(n)[:, :, CHUNK - 1:CHUNK], ACT.Copy)
                    act.activation(a_x2T[b % 2][:, :, 1:], slot_chan(n), ACT.Copy).then_inc(x2T_ready, 1)
                if 0 <= c < CHUNKS:
                    if c == 0:
                        act.wait_ge(rest_loaded, 16 * 15)
                    else:
                        act.wait_ge(parts_stored, 6 * 16 * c)
                    for m, (name, bias, full, parts) in enumerate((("q", "aq", a_qf, a_qp),
                                                                   ("kk", "ak", a_kf, a_kp))):
                        n = take(name, c)
                        for k in range(CT):
                            bias_k = cols[:, COL[bias], k:k + 1]
                            act.activation(full[:, k], slot_chan(n)[:, k], ACT.Identity, bias=bias_k)
                            ins = act.activation(parts[:, 0, k], slot_chan(n)[:, k], ACT.Identity, bias=bias_k)
                        ins.then_inc(part0_ready, 1)
                    for m, (full, parts) in enumerate(((a_qf, a_qp), (a_kf, a_kp))):
                        act.wait_ge(rest1_ready, 2 * c + m + 1)
                        act.activation(parts[:, 1], full, ACT.Copy).then_inc(part1_ready, 1)
            leave(act)

            jobs = 0
            tiles = 0
            for item in ORDER:
                if item[0] == "max":
                    jobs += 1
                elif item[0] == "shift":
                    s = item[1]
                    act.wait_ge(m_full, jobs + 1)
                    src = slot(jobs % 2)[SCORE_ROWS:STACK, 0:CHUNK]
                    for h in range(HG):
                        ins = act.activation(q_stack[SCORE_ROWS:STACK, s % Q_RING, h], src, ACT.Copy)
                    ins.then_inc(shift_placed, 1)
                    jobs += 1
                elif item[0] == "scores":
                    _, s, j, tile, h = item
                    g, c = STEPS[s]
                    q0 = max(0, j - c * TT) * P
                    if tiles == 0:
                        act.wait_ge(phase_a_done, 5)
                    act.wait_ge(scored, tiles + 1)
                    if h == 0 and tile >= 3:
                        act.wait_ge(pv_done, tile - 2)
                    act.activation(probs[:, tile % 3, h, q0:], score_bank[tiles % SCORE_RING][:, q0:],
                                   ACT.Exp, scale=SCALE).then_inc(exp_done, 1)
                    tiles += 1
                elif item[0] == "pv" and item[1] + 1 in last_tile:
                    s = last_tile.index(item[1] + 1)
                    act.wait_ge(pv_done, item[1] + 1)
                    act.activation(oT[:, s % 2], pv_bank, ACT.Copy).then_inc(o_copied, 1)
                elif item[0] == "out":
                    jobs += 1

            def c_take(name, c):
                n = LAST_N[name, c]
                act.wait_ge(c_full, n + 1)
                return n % 4

            for t in range(CHUNKS + 2):
                b = t - 1
                if 0 <= b < CHUNKS:
                    n = c_take("x4T", b)
                    if b:
                        act.wait_ge(c_mix, b)
                    act.activation(c_x4T[(b + 1) % 2][:, :, 0:1], slot_chan(n)[:, :, CHUNK - 1:CHUNK], ACT.Copy)
                    act.activation(c_x4T[b % 2][:, :, 1:], slot_chan(n), ACT.Copy).then_inc(x4T_ready, 1)
                if t < CHUNKS:
                    n = c_take("aT", t)
                    act.activation(c_aT, slot_chan(n), ACT.Copy).then_inc(aT_ready, 1)
                if 0 <= b < CHUNKS:
                    n = c_take("r", b)
                    if b:
                        act.wait_ge(c_out, b)
                    act.activation(c_r, slot_tok(n), ACT.Sigmoid).then_inc(c_r_ready, 1)
                    n = c_take("k", b)
                    act.activation(c_k, slot_chan(n), ACT.Relu).then_inc(c_relu, 1)
                    act.wait_ge(c_relu, b + 1)
                    act.activation(c_k, c_k, ACT.Square).then_inc(c_k2, 1)

        @block.vector
        def _(dve):
            steps = [0]

            def settle(ins):
                steps[0] += 1
                ins.then_inc(dve_step, 1)
                dve.wait_ge(dve_step, steps[0])

            lns = [0]

            def normalize(dst, src, ready, done, first):
                n = lns[0]
                lns[0] += 1
                for k in range(TT):
                    ins = nc.vector.bn_stats(stats[:, k, :], src[:, k, :])
                settle(ins)
                for k in range(TT):
                    ins = nc.vector.bn_aggr(mean_var[:, n % 2, k, :], stats[:, k, :])
                ins.then_inc(ready, 1)
                dve.wait_ge(done, n - first + 1)
                for k in range(TT):
                    ins = nc.vector.tensor_scalar(dst[:, k, :], src[:, k, :], mean_var[:, n % 2, k, 0:1],
                                                  rstd[:, n % 2, k:k + 1], ALU.subtract, ALU.mult)
                return ins

            def take(name, c):
                n = FIRST_N[name, c]
                dve.wait_ge(job_full, n + 1)
                return n % 4

            def mix(x_shifted, xr, xk, ready):
                for dst, mu in ((xr, "mu_r"), (xk, "mu_k")):
                    for k in range(CT):
                        ins = nc.vector.tensor_scalar(dst[:, k], x_shifted[:, k, 1:], cols[:, COL[mu], k:k + 1],
                                                      None, ALU.mult)
                settle(ins)
                for dst, om in ((xr, "om_r"), (xk, "om_k")):
                    for k in range(CT):
                        ins = nc.vector.scalar_tensor_tensor(
                            out=dst[:, k], in0=x_shifted[:, k, 0:CHUNK], scalar=cols[:, COL[om], k:k + 1],
                            in1=dst[:, k], op0=ALU.mult, op1=ALU.add)
                ins.then_inc(ready, 1)

            def over_tokens(v):
                return v[:].rearrange("p (a d) -> p a d", a=1).to_broadcast([P, TT, DIM])

            dve.wait_ge(x_loaded[0], 16)
            normalize(a_xn1[0], a_x[0], stats_ready, rstd_ready, 0).then_inc(xn1_ready, 1)
            dve.wait_ge(rest_loaded, 16 * 15)
            for src, dst in (("mu_r", "om_r"), ("mu_k", "om_k")):
                ins = nc.vector.tensor_scalar(cols[:, COL[dst], :], cols[:, COL[src], :], -1.0, 1.0,
                                              ALU.mult, ALU.add)
            settle(ins)

            for t in range(CHUNKS + 2):
                a, b, c = t, t - 1, t - 2
                if 0 <= b < CHUNKS:
                    n = take("yT", b)
                    if b >= 2:
                        dve.wait_ge(x2_stored, 16 * (b - 1))
                    x1 = a_x1[b % 2]
                    ins = nc.vector.tensor_tensor(x1, a_xn1[b % 2], slot_tok(n), ALU.add)
                    ins.then_inc(z_ready, 1)
                    dve.wait_ge(z_ready, b + 1)
                    settle(normalize(x1, x1, stats_ready, rstd_ready, 0))
                    settle(nc.vector.tensor_tensor(x1, x1, over_tokens(gamma_b), ALU.mult))
                    settle(nc.vector.tensor_tensor(x1, x1, over_tokens(beta_b), ALU.add))
                    nc.vector.tensor_tensor(x1, x1, a_x[b % 3], ALU.add).then_inc(x1_ready, 1)
                    dve.wait_ge(x1_ready, b + 1)
                    normalize(a_xn2, x1, stats_ready, rstd_ready, 0).then_inc(xn2_ready, 1)
                if 0 <= c < CHUNKS:
                    n = take("kv", c)
                    nc.vector.tensor_tensor(a_r, a_r, slot_tok(n), ALU.mult).then_inc(rkv_ready, 1)
                    dve.wait_ge(rkv_ready, c + 1)
                    x2 = a_x1[c % 2]
                    nc.vector.tensor_tensor(x2, x2, a_r, ALU.add).then_inc(x2_ready, 1)
                    dve.wait_ge(x2_ready, c + 1)
                    normalize(a_xn3, x2, stats_ready, rstd_ready, 0).then_inc(xn3_ready, 1)
                if a < CHUNKS:
                    dve.wait_ge(f_ready, a + 1)
                    dve.wait_ge(is_ready, a + 1)
                    for k in range(CT):
                        before = a_h[(a + 1) % 2][:, k, CHUNK - 1:CHUNK] if a else 0.0
                        ins = nc.vector.tensor_tensor_scan(a_h[a % 2][:, k], a_f[:, k], a_i[:, k], before,
                                                           ALU.mult, ALU.add)
                    ins.then_inc(h_ready, 1)
                if 0 <= b < CHUNKS:
                    dve.wait_ge(x2T_ready, b + 1)
                    if b == 0:
                        dve.wait_ge(consts_ready, 5)
                    mix(a_x2T[b % 2], a_xr, a_xk, mix_ready)
                if 0 <= c < CHUNKS:
                    for m, (full, parts) in enumerate(((a_qf, a_qp), (a_kf, a_kp))):
                        dve.wait_ge(part0_ready, 2 * c + m + 1)
                        nc.vector.tensor_tensor(full, full, parts[:, 0], ALU.subtract).then_inc(rest1_ready, 1)
                    n = take("v", c)
                    if c == 0:
                        dve.wait_ge(consts_ready, 5)
                    nc.vector.tensor_tensor(
                        v_aug[:, c * TT:(c + 1) * TT, :, 0:HD],
                        slot_tok(n).rearrange("p t (h d) -> p t h d", d=HD),
                        bv_b[:].rearrange("p (a h d) -> p a h d", a=1, d=HD).to_broadcast([P, TT, HEADS, HD]),
                        ALU.add).then_inc(v_ready, 1)
                if t + 1 < CHUNKS:
                    dve.wait_ge(x_loaded[(t + 1) % 3], 16 * ((t + 1) // 3 + 1))
                    normalize(a_xn1[(t + 1) % 2], a_x[(t + 1) % 3], stats_ready, rstd_ready, 0)\
                        .then_inc(xn1_ready, 1)
            first_lns = lns[0]
            leave(dve)

            dve.wait_ge(part0_ready, 2 * CHUNKS)
            nc.vector.memset(pv_bank, 0.0).then_inc(pv_cleared, 1)
            jobs = reduced = 0
            for item in ORDER:
                if item[0] == "max":
                    _, s, qt, h, k0, k1 = item
                    dve.wait_ge(m_full, jobs + 1)
                    nc.vector.tensor_reduce(span_max[:, s % 2, qt * HG + h, k0 // SPAN:k0 // SPAN + 1],
                                            slot(jobs % 2)[:, 0:k1 - k0], AX.X, ALU.max)\
                        .then_inc(span_reduced, 1)
                    jobs += 1
                    reduced += 1
                    if qt == TT - 1 and h == HG - 1 and k1 == (STEPS[s][1] + 1) * CHUNK:
                        dve.wait_ge(span_reduced, reduced)
                        spans = (k1 + SPAN - 1) // SPAN
                        nm, parts = neg_max, shift_parts[:, s % 2]
                        settle(nc.vector.tensor_reduce(nm[:, 0], span_max[:, s % 2, :, 0:spans], AX.X, ALU.max,
                                                       negate=True))
                        settle(nc.vector.tensor_copy(parts[:, :, 0], nm[:, 0]))
                        settle(nc.vector.tensor_tensor(nm[:, 1], nm[:, 0], parts[:, :, 0], ALU.subtract))
                        settle(nc.vector.tensor_copy(parts[:, :, 1], nm[:, 1]))
                        settle(nc.vector.tensor_tensor(nm[:, 2], nm[:, 1], parts[:, :, 1], ALU.subtract))
                        nc.vector.tensor_copy(parts[:, :, 2], nm[:, 2]).then_inc(shift_ready, 1)
                elif item[0] == "shift":
                    jobs += 1
                elif item[0] == "out":
                    s = item[1]
                    g, c = STEPS[s]
                    if s == 0:
                        dve.wait_ge(phase_a_done, 5)
                        dve.wait_ge(parts_stored, 6 * 16 * CHUNKS)
                    dve.wait_ge(m_full, jobs + 1)
                    o = slot(jobs % 2)[:, 0:CHUNK].rearrange("p (t h d) -> p t h d", t=TT, h=HG)
                    settle(nc.vector.reciprocal(inv_sum[:, s % 2], o[:, :, :, HD]))
                    nc.vector.tensor_tensor(
                        attn[:, c * TT:(c + 1) * TT, g * HG * HD:(g + 1) * HG * HD].rearrange(
                            "p t (h d) -> p t h d", d=HD),
                        o[:, :, :, 0:HD],
                        inv_sum[:, s % 2].rearrange("p t (h a) -> p t h a", a=1).to_broadcast([P, TT, HG, HD]),
                        ALU.mult).then_inc(attn_ready, 1)
                    jobs += 1

            def c_take(name, c):
                n = LAST_N[name, c]
                dve.wait_ge(c_full, n + 1)
                return n % 4

            for t in range(CHUNKS + 2):
                a, b, c = t, t - 1, t - 2
                if 0 <= b < CHUNKS:
                    dve.wait_ge(x4T_ready, b + 1)
                    if b == 0:
                        dve.wait_ge(consts_ready, 6)
                    mix(c_x4T[b % 2], c_xr, c_xk, c_mix)
                if 0 <= c < CHUNKS:
                    n = c_take("kv", c)
                    nc.vector.tensor_tensor(c_r, c_r, slot_tok(n), ALU.mult).then_inc(c_rkv, 1)
                    dve.wait_ge(c_rkv, c + 1)
                    nc.vector.tensor_tensor(c_x[c % 4], c_x[c % 4], c_r, ALU.add).then_inc(c_out, 1)
                if a < CHUNKS:
                    x3 = c_x[a % 4]
                    dve.wait_ge(c_loaded[a % 4], 16 * (a // 4 + 1))
                    settle(nc.vector.tensor_tensor(x3, x3, over_tokens(bo_b), ALU.add))
                    n = c_take("proj", a)
                    nc.vector.tensor_tensor(x3, x3, slot_tok(n), ALU.add).then_inc(c_x3, 1)
                    dve.wait_ge(c_x3, a + 1)
                    normalize(c_xn4, x3, c_stats, c_rstd, first_lns).then_inc(xn4_ready, 1)

        @block.tensor
        def _(pe):
            FIRST_READ = {"yT": z_ready, "r": r_ready, "k": relu_ready, "x1T": x1T_ready, "kv": rkv_ready,
                          "f": f_ready, "i": i_ready, "s": s_ready, "o": o_ready, "x3T": x3T_ready,
                          "x2T": x2T_ready, "q": part0_ready, "kk": part0_ready, "v": v_ready}
            LAST_READ = {"x4T": x4T_ready, "aT": aT_ready, "kv": c_rkv, "proj": c_x3, "r": c_r_ready,
                         "k": c_relu}

            def claim(m, jobs, read):
                if m >= 4:
                    name, c = jobs[m - 4]
                    pe.wait_ge(read[name], {"q": 2 * c + 1, "kk": 2 * c + 2}.get(name, c + 1))
                return m % 4

            def to_channels(n, src):
                for k in range(CT):
                    for j in range(TT):
                        ins = nc.tensor.transpose(slot_chan(n)[:, k, j * P:(j + 1) * P],
                                                  src[:, j, k * P:(k + 1) * P], ident[:])
                return ins

            def channels_out(n, w, src):
                for e in range(CT):
                    for k in range(CT):
                        ins = nc.tensor.matmul(slot_chan(n)[:, e], w[:, k, e * P:(e + 1) * P], src[:, k],
                                               start=(k == 0), stop=(k == CT - 1))
                return ins

            def tokens_out(n, w, src):
                for j in range(TT):
                    for k in range(CT):
                        ins = nc.tensor.matmul(slot_tok(n)[:, j], src[:, k, j * P:(j + 1) * P], w[:, k],
                                               start=(k == 0), stop=(k == CT - 1))
                return ins

            pe.wait_ge(consts_ready, 3)
            for m, (name, c) in enumerate(FIRST):
                n = claim(m, FIRST, FIRST_READ)
                if name == "yT":
                    pe.wait_ge(y_ready, c + 1)
                    for j in range(TT):
                        for k in range(CT):
                            ins = nc.tensor.transpose(slot_tok(n)[:, j, k * P:(k + 1) * P],
                                                      a_o[:, k, j * P:(j + 1) * P], ident[:])
                elif name == "r":
                    pe.wait_ge(mix_ready, c + 1)
                    if c == 0:
                        pe.wait_ge(rest_loaded, 16 * 15)
                    ins = tokens_out(n, weights["r"], a_xr)
                elif name == "k":
                    ins = channels_out(n, weights["k"], a_xk)
                elif name == "x1T":
                    pe.wait_ge(xn1_ready, c + 1)
                    ins = to_channels(n, a_xn1[c % 2])
                elif name == "kv":
                    pe.wait_ge(k2_ready, c + 1)
                    ins = tokens_out(n, weights["v"], a_k)
                elif name in ("f", "i", "s", "o"):
                    if name == "f":
                        pe.wait_ge(x1T_ready, c + 1)
                        pe.wait_ge(gates_loaded, 16 * 8)
                    ins = channels_out(n, weights[name], a_x1T)
                elif name == "x3T":
                    pe.wait_ge(xn3_ready, c + 1)
                    ins = to_channels(n, a_xn3)
                elif name == "x2T":
                    pe.wait_ge(xn2_ready, c + 1)
                    ins = to_channels(n, a_xn2)
                elif name == "q":
                    pe.wait_ge(x3T_ready, c + 1)
                    ins = channels_out(n, weights["aq"], a_x3T)
                elif name == "kk":
                    ins = channels_out(n, weights["ak"], a_x3T)
                elif name == "v":
                    ins = tokens_out(n, weights["av"], a_x3T)
                ins.then_inc(job_full, 1)
            leave(pe)
            pe.wait_ge(part0_ready, 2 * CHUNKS)
            pe.wait_ge(v_ready, CHUNKS)

            scores = 0
            q_seen, k_seen = -1, -1

            reads = []
            spans_sent = 0

            def claim_m(read, value):
                if len(reads) >= 2:
                    pe.wait_ge(*reads[-2])
                reads.append((read, value))
                return (len(reads) - 1) % 2

            for item in ORDER:
                if item[0] == "max":
                    _, s, qt, h, k0, k1 = item
                    g, c = STEPS[s]
                    spans_sent += 1
                    n = claim_m(span_reduced, spans_sent)
                    if s != q_seen:
                        q_seen = s
                        pe.wait_ge(q_loaded[s % Q_RING], 16 * len(Q_PARTS) * (s // Q_RING + 1))
                    if (g, c) != k_seen:
                        k_seen = (g, c)
                        if g == 0:
                            b, chunks = {0: (0, 1), CHUNKS - 1: (1, 1)}.get(c, (3, CHUNKS - 2))
                            pe.wait_ge(k_loaded[b], 16 * len(K_PARTS) + 16 * chunks)
                        elif g == 1:
                            pe.wait_ge(k_loaded[2], 16 * len(K_PARTS) + 16 * CHUNKS)
                        else:
                            pe.wait_ge(k_loaded[g % 2], 16 * len(K_PARTS) * 2 + 16)
                    for a in range(k0, k1, CHUNK):
                        b = min(a + CHUNK, k1)
                        ends = b == (c * TT + qt + 1) * P
                        ins = nc.tensor.matmul(slot(n)[:, a - k0:b - k0],
                                               q_stack[0:SCORE_ROWS, s % Q_RING, h, qt * P:(qt + 1) * P],
                                               k_stack[0:SCORE_ROWS, g % 2, h, a:b], start=True, stop=not ends)
                        if ends:
                            ins = nc.tensor.matmul(slot(n)[:, b - P - k0:b - k0], ident_b[:], mask_b[:],
                                                   start=False, stop=True)
                    ins.then_inc(m_full, 1)
                elif item[0] == "shift":
                    s = item[1]
                    n = claim_m(shift_placed, s + 1)
                    pe.wait_ge(shift_ready, s + 1)
                    for qt in range(TT):
                        ins = nc.tensor.matmul(
                            slot(n)[SCORE_ROWS:STACK, qt * P:(qt + 1) * P],
                            shift_parts[:, s % 2, qt * HG:(qt + 1) * HG, :].rearrange("p h r -> p (h r)"),
                            ident_b[:], start=True, stop=True)
                    ins.then_inc(m_full, 1)
                elif item[0] == "scores":
                    _, s, j, tile, h = item
                    g, c = STEPS[s]
                    q0 = max(0, j - c * TT) * P
                    if j == 0 and h == 0:
                        pe.wait_ge(shift_placed, s + 1)
                    if scores >= SCORE_RING:
                        pe.wait_ge(exp_done, scores - SCORE_RING + 1)
                    nc.tensor.matmul(score_bank[scores % SCORE_RING][:, q0:],
                                     k_stack[0:STACK, g % 2, h, j * P:(j + 1) * P],
                                     q_stack[0:STACK, s % Q_RING, h, q0:], start=True, stop=True).then_inc(scored, 1)
                    scores += 1
                elif item[0] == "pv":
                    tile = item[1]
                    s = next(k for k, e in enumerate(last_tile) if tile < e)
                    g, c = STEPS[s]
                    j = tile - (last_tile[s] - TT * (c + 1))
                    d = j - c * TT
                    if d >= 0:
                        pe.wait_ge(masked, s * TT + d + 1)
                    else:
                        pe.wait_ge(exp_done, HG * (tile + 1))
                    if j == 0:
                        if s == 0:
                            pe.wait_ge(pv_cleared, 1)
                        else:
                            pe.wait_ge(o_copied, s)
                    q0 = max(0, d) * P
                    for h in range(HG):
                        ins = nc.tensor.matmul(pv_bank[32 * h:32 * h + VW, q0:], v_aug[:, j, g * HG + h, :],
                                               probs[:, tile % 3, h, q0:], start=(j == 0),
                                               stop=(j == TT * (c + 1) - 1))
                    ins.then_inc(pv_done, 1)
                elif item[0] == "out":
                    s = item[1]
                    n = claim_m(attn_ready, s + 1)
                    pe.wait_ge(o_copied, s + 1)
                    for qt in range(TT):
                        ins = nc.tensor.transpose(slot(n)[:, qt * P:(qt + 1) * P],
                                                  oT[:, s % 2, qt * P:(qt + 1) * P], ident[:])
                    ins.then_inc(m_full, 1)
            pe.wait_ge(attn_ready, len(STEPS))

            for m, (name, c) in enumerate(LAST):
                n = claim(m, LAST, LAST_READ)
                if name == "x4T":
                    pe.wait_ge(xn4_ready, c + 1)
                    ins = to_channels(n, c_xn4)
                elif name == "aT":
                    ins = to_channels(n, attn[:, c * TT:(c + 1) * TT, :])
                elif name == "kv":
                    pe.wait_ge(c_k2, c + 1)
                    ins = tokens_out(n, weights["v"], c_k)
                elif name == "proj":
                    pe.wait_ge(aT_ready, c + 1)
                    ins = tokens_out(n, weights["ao"], c_aT)
                elif name == "r":
                    pe.wait_ge(c_mix, c + 1)
                    ins = tokens_out(n, weights["r"], c_xr)
                elif name == "k":
                    ins = channels_out(n, weights["k"], c_xk)
                ins.then_inc(c_full, 1)


_INS = ["x", "Wi", "bi", "Wf", "bf", "Wo_gate", "bo_gate", "Ws", "bs", "gamma", "beta", "WqT", "bq", "WkT", "bk",
        "WvT", "bv", "WoT", "bo", "WrT", "WkfT", "WvfT", "mu_r", "mu_k"]


def kernel(L0_attn_a_x, L0_attn_a_Wi, L0_attn_a_bi, L0_attn_a_Wf, L0_attn_a_bf, L0_attn_a_Wo, L0_attn_a_bo,
           L0_attn_a_Ws, L0_attn_a_bs, L0_attn_a_gamma, L0_attn_a_beta, L0_attn_b_Wq, L0_attn_b_bq, L0_attn_b_Wk,
           L0_attn_b_bk, L0_attn_b_Wv, L0_attn_b_bv, L0_attn_b_Wo, L0_attn_b_bo, L0_ffn_W_r, L0_ffn_W_k,
           L0_ffn_W_v, L0_ffn_mu_r, L0_ffn_mu_k):
    from concourse import bacc
    from concourse.bass_utils import run_bass_kernel_spmd

    given = [L0_attn_a_x.reshape(TOKENS, DIM), L0_attn_a_Wi, L0_attn_a_bi, L0_attn_a_Wf, L0_attn_a_bf,
             L0_attn_a_Wo, L0_attn_a_bo, L0_attn_a_Ws, L0_attn_a_bs, L0_attn_a_gamma, L0_attn_a_beta,
             L0_attn_b_Wq.T, L0_attn_b_bq, L0_attn_b_Wk.T, L0_attn_b_bk, L0_attn_b_Wv.T, L0_attn_b_bv,
             L0_attn_b_Wo.T, L0_attn_b_bo, L0_ffn_W_r.T, L0_ffn_W_k.T, L0_ffn_W_v.T, L0_ffn_mu_r, L0_ffn_mu_k]
    nc = bacc.Bacc("TRN2", target_bir_lowering=False, num_devices=1)
    arrays, args = {}, []
    for name, a in zip(_INS, given):
        a = np.ascontiguousarray(a)
        arrays[f"in_{name}"] = a
        args.append(nc.dram_tensor(f"in_{name}", a.shape, mybir.dt.from_np(a.dtype), kind="ExternalInput").ap())
    out = nc.dram_tensor("out", (TOKENS, DIM), F32, kind="ExternalOutput").ap()
    build(nc, *args, out)
    result = run_bass_kernel_spmd(nc, [arrays], core_ids=[0])
    return result.results[0]["out"].reshape(1, TOKENS, DIM)
```
